# Optimizing a Trainium2 kernel written in Bass

```python
import numpy as np
import jax
import jax.numpy as jnp

def _softmax(x, axis=-1):
    return jax.nn.softmax(x, axis=axis)

def _gelu(x):
    return jax.nn.gelu(x, approximate=True)

def _silu(x):
    return jax.nn.silu(x)

def _sigmoid(x):
    return jax.nn.sigmoid(x)

def _layernorm(x, axis=-1, eps=1e-05):
    m = jnp.mean(x, axis=axis, keepdims=True)
    v = jnp.var(x, axis=axis, keepdims=True)
    return (x - m) / jnp.sqrt(v + eps)

def _scatter_add(tgt, idx, src, axis=0):
    return tgt.at[idx].add(src)

def _segment_sum(src, seg, n):
    return jax.ops.segment_sum(src, seg, n)
kernel_name = 'mk_seq_postln_d1_jaxref_r8_f89119'

def setup_inputs(seed: int=0):
    np.random.seed(seed)
    _w = jnp.asarray

    def _L0_attn_setup():
        import jax, jax.numpy as jnp
        import numpy as np
        from jax import lax
        B, T, D, H, K = (4, 256, 128, 512, 3)
        EPS = 1e-06

        def _rmsnorm(z, w):
            return z * lax.rsqrt(jnp.mean(z * z, axis=-1, keepdims=True) + EPS) * w
        key = jax.random.key(seed)
        ks = jax.random.split(key, 12)
        return {'x': jax.random.normal(ks[0], (B, T, D), jnp.float32), 'norm_w': jnp.ones((D,), jnp.float32), 'conv_w': jax.random.normal(ks[1], (D, 1, K), jnp.float32) * 0.1, 'conv_b': jax.random.normal(ks[2], (D,), jnp.float32) * 0.01, 'a': jnp.tanh(jax.random.normal(ks[3], (D,), jnp.float32)), 'b': jax.random.normal(ks[4], (D,), jnp.float32), 'mlp_norm_w': jnp.ones((D,), jnp.float32), 'w_gate': jax.random.normal(ks[5], (D, H), jnp.float32) * D ** (-0.5), 'b_gate': jnp.zeros((H,), jnp.float32), 'w_up': jax.random.normal(ks[6], (D, H), jnp.float32) * D ** (-0.5), 'b_up': jnp.zeros((H,), jnp.float32), 'w_down': jax.random.normal(ks[7], (H, D), jnp.float32) * H ** (-0.5), 'b_down': jnp.zeros((D,), jnp.float32)}
    _L0_attn_in = _L0_attn_setup()

    def _L0_ffn_setup():
        import jax, jax.numpy as jnp
        import numpy as np
        H = 128
        I = 88
        E = 64
        TOP_K = 8
        NG = 8
        TOPK_GROUP = 4
        N_SHARED = 2
        ROUTED_SCALE = 2.5
        S_I = I * N_SHARED

        def _route(x, gate_w, gate_bias):
            T = x.shape[0]
            logits = x @ gate_w.T
            scores = jax.nn.sigmoid(logits)
            scores_for_choice = scores + gate_bias[None, :]
            grp = scores_for_choice.reshape(T, NG, E // NG)
            group_scores = jnp.sum(jax.lax.top_k(grp, 2)[0], axis=-1)
            _, gidx = jax.lax.top_k(group_scores, TOPK_GROUP)
            gmask = jnp.zeros((T, NG), dtype=scores.dtype).at[jnp.arange(T)[:, None], gidx].set(1.0)
            emask = jnp.repeat(gmask, E // NG, axis=1)
            masked = jnp.where(emask > 0, scores_for_choice, 0.0)
            _, topk_idx = jax.lax.top_k(masked, TOP_K)
            topk_w = jnp.take_along_axis(scores, topk_idx, axis=1)
            topk_w = topk_w / (jnp.sum(topk_w, axis=-1, keepdims=True) + 1e-20)
            topk_w = topk_w * ROUTED_SCALE
            rw = jnp.zeros((T, E), dtype=scores.dtype).at[jnp.arange(T)[:, None], topk_idx].add(topk_w)
            return rw

        def _mlp(x, gw, uw, dw):
            return jax.nn.silu(x @ gw.T) * (x @ uw.T) @ dw.T
        key = jax.random.key(seed)
        ks = jax.random.split(key, 10)
        sc = 0.02
        return {'hidden_states': jax.random.normal(ks[0], (1, 128, H), dtype=jnp.float32), 'gate_w': sc * jax.random.normal(ks[1], (E, H), dtype=jnp.float32), 'gate_bias': sc * jax.random.normal(ks[2], (E,), dtype=jnp.float32), 'Wg': sc * jax.random.normal(ks[3], (E, I, H), dtype=jnp.float32), 'Wu': sc * jax.random.normal(ks[4], (E, I, H), dtype=jnp.float32), 'Wd': sc * jax.random.normal(ks[5], (E, H, I), dtype=jnp.float32), 'Sg': sc * jax.random.normal(ks[6], (S_I, H), dtype=jnp.float32), 'Su': sc * jax.random.normal(ks[7], (S_I, H), dtype=jnp.float32), 'Sd': sc * jax.random.normal(ks[8], (H, S_I), dtype=jnp.float32)}
    _L0_ffn_in = _L0_ffn_setup()
    _d = {'L0_attn_x': _L0_attn_in['x'], 'L0_attn_norm_w': _L0_attn_in['norm_w'], 'L0_attn_conv_w': _L0_attn_in['conv_w'], 'L0_attn_conv_b': _L0_attn_in['conv_b'], 'L0_attn_a': _L0_attn_in['a'], 'L0_attn_b': _L0_attn_in['b'], 'L0_attn_mlp_norm_w': _L0_attn_in['mlp_norm_w'], 'L0_attn_w_gate': _L0_attn_in['w_gate'], 'L0_attn_b_gate': _L0_attn_in['b_gate'], 'L0_attn_w_up': _L0_attn_in['w_up'], 'L0_attn_b_up': _L0_attn_in['b_up'], 'L0_attn_w_down': _L0_attn_in['w_down'], 'L0_attn_b_down': _L0_attn_in['b_down'], 'L0_ffn_gate_w': _L0_ffn_in['gate_w'], 'L0_ffn_gate_bias': _L0_ffn_in['gate_bias'], 'L0_ffn_Wg': _L0_ffn_in['Wg'], 'L0_ffn_Wu': _L0_ffn_in['Wu'], 'L0_ffn_Wd': _L0_ffn_in['Wd'], 'L0_ffn_Sg': _L0_ffn_in['Sg'], 'L0_ffn_Su': _L0_ffn_in['Su'], 'L0_ffn_Sd': _L0_ffn_in['Sd']}
    _x0 = _d['L0_attn_x']
    _d['L0_attn_x'] = jax.random.normal(jax.random.fold_in(jax.random.key(seed), 1), (4, 1024, 128), dtype=_x0.dtype)
    del _x0
    return _d

def reference(L0_attn_x, L0_attn_norm_w, L0_attn_conv_w, L0_attn_conv_b, L0_attn_a, L0_attn_b, L0_attn_mlp_norm_w, L0_attn_w_gate, L0_attn_b_gate, L0_attn_w_up, L0_attn_b_up, L0_attn_w_down, L0_attn_b_down, L0_ffn_gate_w, L0_ffn_gate_bias, L0_ffn_Wg, L0_ffn_Wu, L0_ffn_Wd, L0_ffn_Sg, L0_ffn_Su, L0_ffn_Sd):

    def _L0_attn_ref(x, norm_w, conv_w, conv_b, a, b, mlp_norm_w, w_gate, b_gate, w_up, b_up, w_down, b_down):
        import jax, jax.numpy as jnp
        import numpy as np
        from jax import lax
        B, T, D, H, K = (4, 256, 128, 512, 3)
        EPS = 1e-06

        def _rmsnorm(z, w):
            return z * lax.rsqrt(jnp.mean(z * z, axis=-1, keepdims=True) + EPS) * w
        y = _rmsnorm(x, norm_w)
        y_conv = lax.conv_general_dilated(y.transpose(0, 2, 1), conv_w, window_strides=(1,), padding=[(K // 2, K // 2)], dimension_numbers=('NCH', 'OIH', 'NCH'), feature_group_count=D) + conv_b[None, :, None]
        y_conv = y_conv.transpose(0, 2, 1)
        s = jnp.tanh(a)
        by = b * y

        def step(h, by_t):
            h = s * h + by_t
            return (h, h)
        _, y_ssm = lax.scan(step, jnp.zeros((x.shape[0], x.shape[2]), x.dtype), by.transpose(1, 0, 2))
        y_ssm = y_ssm.transpose(1, 0, 2)
        x = x + y_conv + y_ssm
        z = _rmsnorm(x, mlp_norm_w)
        h = jax.nn.silu(z @ w_gate + b_gate) * (z @ w_up + b_up)
        return x + h @ w_down + b_down

    def _L0_ffn_ref(hidden_states, gate_w, gate_bias, Wg, Wu, Wd, Sg, Su, Sd):
        import jax, jax.numpy as jnp
        import numpy as np
        H = 128
        I = 88
        E = 64
        TOP_K = 8
        NG = 8
        TOPK_GROUP = 4
        N_SHARED = 2
        ROUTED_SCALE = 2.5
        S_I = I * N_SHARED

        def _route(x, gate_w, gate_bias):
            T = x.shape[0]
            logits = x @ gate_w.T
            scores = jax.nn.sigmoid(logits)
            scores_for_choice = scores + gate_bias[None, :]
            grp = scores_for_choice.reshape(T, NG, E // NG)
            group_scores = jnp.sum(jax.lax.top_k(grp, 2)[0], axis=-1)
            _, gidx = jax.lax.top_k(group_scores, TOPK_GROUP)
            gmask = jnp.zeros((T, NG), dtype=scores.dtype).at[jnp.arange(T)[:, None], gidx].set(1.0)
            emask = jnp.repeat(gmask, E // NG, axis=1)
            masked = jnp.where(emask > 0, scores_for_choice, 0.0)
            _, topk_idx = jax.lax.top_k(masked, TOP_K)
            topk_w = jnp.take_along_axis(scores, topk_idx, axis=1)
            topk_w = topk_w / (jnp.sum(topk_w, axis=-1, keepdims=True) + 1e-20)
            topk_w = topk_w * ROUTED_SCALE
            rw = jnp.zeros((T, E), dtype=scores.dtype).at[jnp.arange(T)[:, None], topk_idx].add(topk_w)
            return rw

        def _mlp(x, gw, uw, dw):
            return jax.nn.silu(x @ gw.T) * (x @ uw.T) @ dw.T
        B, S, _ = hidden_states.shape
        x = hidden_states.reshape(B * S, H)
        rw = _route(x, gate_w, gate_bias)
        expert_out = jax.vmap(lambda gw_, uw_, dw_: _mlp(x, gw_, uw_, dw_))(Wg, Wu, Wd)
        routed = jnp.einsum('eth,te->th', expert_out, rw)
        shared = _mlp(x, Sg, Su, Sd)
        out = (routed + shared).reshape(B, S, H)
        return out
    x = L0_attn_x
    x = _layernorm(x + _L0_attn_ref(x, L0_attn_norm_w, L0_attn_conv_w, L0_attn_conv_b, L0_attn_a, L0_attn_b, L0_attn_mlp_norm_w, L0_attn_w_gate, L0_attn_b_gate, L0_attn_w_up, L0_attn_b_up, L0_attn_w_down, L0_attn_b_down), axis=-1)
    x = _layernorm(x + _L0_ffn_ref(x, L0_ffn_gate_w, L0_ffn_gate_bias, L0_ffn_Wg, L0_ffn_Wu, L0_ffn_Wd, L0_ffn_Sg, L0_ffn_Su, L0_ffn_Sd), axis=-1)
    return x

_drawn_inputs = setup_inputs


def setup_inputs(seed=0):
    import zlib

    import numpy as np

    out = dict(_drawn_inputs(seed))
    spreads = {'L0_attn_norm_w': (1.0, 0.2),
     'L0_attn_mlp_norm_w': (1.0, 0.2),
     'L0_attn_b_gate': (0.0, 0.302),
     'L0_attn_b_up': (0.0, 0.294),
     'L0_attn_b_down': (0.0, 0.1)}
    factors = {'L0_attn_conv_b': 8.0,
     'L0_ffn_gate_w': 8.0,
     'L0_ffn_gate_bias': 8.0,
     'L0_ffn_Wg': 8.0,
     'L0_ffn_Wu': 8.0,
     'L0_ffn_Wd': 8.0,
     'L0_ffn_Sg': 8.0,
     'L0_ffn_Su': 8.0,
     'L0_ffn_Sd': 8.0}
    for name, (base, spread) in spreads.items():
        noise = np.random.default_rng([zlib.crc32(name.encode()), seed]).standard_normal(out[name].shape)
        drawn = base * np.exp(spread * noise) if base else spread * noise
        out[name] = jnp.asarray(drawn.astype(out[name].dtype))
    for name, factor in factors.items():
        out[name] = (out[name] * factor).astype(out[name].dtype)
    return out
```

```python
from contextlib import ExitStack

import concourse.bass as bass
from concourse import mybir

F32 = mybir.dt.float32
BF16 = mybir.dt.bfloat16
I32 = mybir.dt.int32
U32 = mybir.dt.uint32
ALU = mybir.AluOpType
ACT = mybir.ActivationFunctionType
AX_X = mybir.AxisListType.X

P = 128
NB = 4
T = 1024
NT = T // P
HID = 512
NM = HID // P
E = 64
I = 88
K = 8
NG = 8
EG = E // NG
TOPG = 4
SJ = 2
ROUTED_SCALE = 2.5
RMS_EPS = 1e-6
LN_EPS = 1e-5
BIG = 1e30
GONE = -3e38
ET = T * K // P + E
SLOTS = ET * P
QUAD = 4
NQ = ET // QUAD
UN = 4
OCT = 2 * QUAD

V_NORM, V_CW, V_CB, V_A, V_B, V_MN, V_BG, V_BU = 0, 1, 4, 5, 6, 7, 8, 8 + NM
NV = 8 + 2 * NM


def build(nc, x, vecs, w_gate, w_up, w_down, b_down, gate_wT, gate_bias, wgu, wd, sgu, sd, out, xs, os):
    with ExitStack() as ctx:
        def sb(name, shape, dt=F32):
            return ctx.enter_context(nc.sbuf_tensor(name, shape, dt))

        def psum(name, shape, dt=F32):
            return ctx.enter_context(nc.psum_tensor(name, shape, dt))

        def sem(name):
            return ctx.enter_context(nc.semaphore(name))

        wgu_sb = sb("wgu_sb", [P, E, 2 * I])
        wd_sb = sb("wd_sb", [I, E, P])
        wgate_sb = sb("wgate_sb", [P, HID])
        wup_sb = sb("wup_sb", [P, HID])
        wdown_sb = sb("wdown_sb", [P, NM, P])
        bdown_sb = sb("bdown_sb", [1, P])
        gatew_sb = sb("gatew_sb", [P, E])
        gbias_sb = sb("gbias_sb", [P, E])
        sgu_sb = sb("sgu_sb", [P, 2, SJ, I])
        sd_sb = sb("sd_sb", [I, SJ, P])
        vec = sb("vec", [P, NV])
        tanh_a = sb("tanh_a", [P, 1])
        eps = sb("eps", [P, 2])
        ident = sb("ident", [P, P])
        ones = sb("ones", [P, P])
        ident_bf = sb("ident_bf", [P, P], BF16)
        ones_bf = sb("ones_bf", [P, P], BF16)
        before_bf = sb("before_bf", [P, P], BF16)
        lower_g = sb("lower_g", [P, NG, NG])
        iota_i = sb("iota_i", [P, 1], I32)
        iota_f = sb("iota_f", [P, 1])

        x_all = sb("x_all", [P, NB * NT, P])
        x1r = sb("x1r", [P, 2 * NT, P])
        slots = sb("slots", [P, NB, NT * K], U32)
        wk = sb("wk", [P, NB, NT * K])
        gbuf = sb("gbuf", [P, NT, K, P])

        work_a = sb("work_a", [P, T])
        work_b = sb("work_b", [P, T])
        yT = sb("yT", [P, T + 2])
        x2T = sb("x2T", [P, T])
        zT = sb("zT", [P, T])
        gbuf2 = sb("gbuf2", [P, 2, 512])
        h_sb = sb("h_sb", [P, 4, 512])
        rw = sb("rw", [P, NT, E])
        key = sb("key", [P, NT, E])
        sel = sb("sel", [P, NT, E], BF16)
        ss = sb("ss", [P, 3, NT])
        rs = sb("rs", [P, 3, NT])
        stats = sb("stats", [P, NT, 6])
        mv = sb("mv", [P, NT, 2])
        small = sb("small", [P, 6, E])
        keys = sb("keys", [P, NT, K])
        top = sb("top", [P, NT, K])
        wsum = sb("wsum", [P, 2, NT])
        cnt_i = sb("cnt_i", [P, 2, E], I32)
        tiles = sb("tiles", [P, 3, E])
        eid_col = sb("eid_col", [P, 3])
        eid_bf = sb("eid_bf", [P, 1], BF16)
        eid = sb("eid", [1, 2, ET], I32)
        xl = sb("xl", [P, 2, OCT, P])
        ol = sb("ol", [P, 2, OCT, P])
        cst = sb("cst", [P, 4, 6])
        cmv = sb("cmv", [P, 4, 2])
        csd = sb("csd", [P, 2, 4])

        score = work_b[:, 0:512].rearrange("p (t e) -> p t e", e=E)
        choice = work_b[:, 512:1024].rearrange("p (t e) -> p t e", e=E)
        tab_a = work_a[:, 0:512].rearrange("p (t e) -> p t e", e=E)
        tab_b = work_a[:, 512:1024].rearrange("p (t e) -> p t e", e=E)
        xg = gbuf2
        hT = zT[:, :].rearrange("p (r c) -> p r c", r=2)
        eg = h_sb[:, 0:2, 0:QUAD * I]
        eh = h_sb[:, 2:4, 0:QUAD * I]
        hs = h_sb[:, :, :].rearrange("p (j a) c -> p j (a c)", j=SJ)

        GU = psum("GU", [P, 4, 512])
        XT = psum("XT", [P, 512])
        HT = psum("HT", [P, 512])
        OT = psum("OT", [P, 512])
        MI = psum("MI", [P, 512])
        gu_flat = GU[:, :, :].rearrange("p b c -> p (b c)")

        s_par = sem("s_par")
        s_mlpw = sem("s_mlpw")
        s_shw = sem("s_shw")
        s_expw = sem("s_expw")
        d_x = [sem(f"d_x{b}") for b in range(NB)]
        s_zero = sem("s_zero")
        s_fill = [sem(f"s_fill{r}") for r in range(2)]
        s_const = sem("s_const")
        s_cdve = sem("s_cdve")
        s_cact = sem("s_cact")
        dv = sem("dv")
        s_sqx = sem("s_sqx")
        s_ssx = sem("s_ssx")
        s_sdx = sem("s_sdx")
        s_yr = sem("s_yr")
        p_xT = sem("p_xT")
        p_yT = sem("p_yT")
        s_xT = sem("s_xT")
        s_yT = sem("s_yT")
        s_x2 = sem("s_x2")
        s_sq2 = sem("s_sq2")
        p_ss2 = sem("p_ss2")
        s_sd2 = sem("s_sd2")
        s_diag = sem("s_diag")
        p_rs = sem("p_rs")
        s_z = sem("s_z")
        p_gu = sem("p_gu")
        s_sil = sem("s_sil")
        s_h = sem("s_h")
        p_dn = sem("p_dn")
        s_v = sem("s_v")
        s_mv = sem("s_mv")
        s_sd3 = sem("s_sd3")
        s_x1r = sem("s_x1r")
        p_x1 = sem("p_x1")
        s_x1T = sem("s_x1T")
        p_lg = sem("p_lg")
        s_sc = sem("s_sc")
        s_sel = sem("s_sel")
        p_rank = sem("p_rank")
        s_slot = sem("s_slot")
        s_ecol = sem("s_ecol")
        p_erow = sem("p_erow")
        s_eid = sem("s_eid")
        s_wk = sem("s_wk")
        p_sh = sem("p_sh")
        s_ssil = sem("s_ssil")
        s_sh = sem("s_sh")
        p_sd = sem("p_sd")
        s_res = sem("s_res")
        d_scat = [sem(f"d_scat{b}") for b in range(NB)]
        d_ld = [sem(f"d_ld{r}") for r in range(2)]
        d_st = [sem(f"d_st{r}") for r in range(2)]
        d_gat = [[sem(f"d_gat{b}_{h}") for h in range(2)] for b in range(NB)]
        p_tx = sem("p_tx")
        s_xg = sem("s_xg")
        p_eg = sem("p_eg")
        s_eg = sem("s_eg")
        s_eh = sem("s_eh")
        p_th = sem("p_th")
        s_ht = sem("s_ht")
        p_eo = sem("p_eo")
        s_eo = sem("s_eo")
        s_acc = sem("s_acc")
        s_cmv = sem("s_cmv")
        s_csd = sem("s_csd")
        s_out = sem("s_out")
        d_out = sem("d_out")

        xs_t = [xs[r].rearrange("(n p) d -> p n d", p=P) for r in range(2)]
        os_t = [os[r].rearrange("(n p) d -> p n d", p=P) for r in range(2)]
        phases = [("A", 0), ("A", 1), ("E", 0), ("A", 2), ("E", 1), ("C", 0), ("A", 3), ("E", 2), ("C", 1),
                  ("E", 3), ("C", 2), ("C", 3)]

        def a_before_e(b):
            return min(b + 2, NB)

        def e_before_a(b):
            return max(b - 1, 0)

        def quads(step):
            def run(eng, b):
                for q in range(UN):
                    step(b, q, q)
                with eng.Fori(1, NQ // UN - 1) as i:
                    for u in range(UN):
                        step(b, i * UN + u, u)
                for q in range(NQ - UN, NQ):
                    step(b, q, q)
            return run

        def has(b, q, n):
            return not isinstance(q, int) or NQ * b + q >= n

        block = ctx.enter_context(nc.Block())

        @block.sync
        def _(sp):
            def fill(r):
                zeros = gbuf[:, 0, :, :].rearrange("p k d -> p (k d)")
                dst = xs[r].rearrange("(p n c) d -> p n (c d)", p=P, c=K)
                sp.dma_start(dst, zeros.unsqueeze(1).to_broadcast([P, ET // K, K * P])).then_inc(s_fill[r], 16)

            sp.dma_start(x_all[:, 0:NT, :], x[0].rearrange("(t p) d -> p t d", p=P)).then_inc(d_x[0], 16)
            sp.dma_start(vec[:, :], vecs).then_inc(s_par, 16)
            sp.dma_start(bdown_sb[:, :], b_down).then_inc(s_par, 16)
            sp.dma_start(wgate_sb[:, :], w_gate).then_inc(s_mlpw, 16)
            sp.dma_start(wup_sb[:, :], w_up).then_inc(s_mlpw, 16)
            sp.dma_start(wdown_sb[:, :, :], w_down.rearrange("(m p) d -> p m d", p=P)).then_inc(s_mlpw, 16)
            sp.dma_start(gatew_sb[:, :], gate_wT).then_inc(s_shw, 16)
            sp.dma_start(gbias_sb[:, :], gate_bias.partition_broadcast(P)).then_inc(s_shw, 16)
            sp.dma_start(sgu_sb[:, :, :, :], sgu).then_inc(s_shw, 16)
            sp.dma_start(sd_sb[:, :, :], sd).then_inc(s_shw, 16)
            sp.wait_ge(s_zero, 1)
            fill(0)
            for b in range(1, NB):
                sp.dma_start(x_all[:, b * NT:(b + 1) * NT, :], x[b].rearrange("(t p) d -> p t d", p=P)).then_inc(d_x[b], 16)
            sp.dma_start(wgu_sb[:, :, :], wgu).then_inc(s_expw, 16)
            sp.dma_start(wd_sb[:, :, :], wd).then_inc(s_expw, 16)
            fill(1)

            def load(b, o, u):
                sp.dma_start(xl[:, u, :, :], xs_t[b % 2][:, bass.ds(o * OCT, OCT), :]).then_inc(d_ld[u], 16)

            def store(b, o, u):
                sp.wait_ge(s_eo, NQ * b + 2 * o + 2)
                sp.dma_start(os_t[b % 2][:, bass.ds(o * OCT, OCT), :], ol[:, u, :, :]).then_inc(d_st[u], 16)

            NO = NQ // 2

            def experts(b):
                sp.wait_ge(d_scat[b], 16 * NT * K)
                if b >= 2:
                    for h in range(2):
                        sp.wait_ge(d_gat[b - 2][h], 16 * NT * K // 2)
                for u in range(2):
                    if b:
                        sp.wait_ge(p_tx, NQ * b)
                    load(b, u, u)
                with sp.Fori(0, NO // 2 - 1) as i:
                    for u in range(2):
                        o = i * 2 + u
                        sp.wait_ge(p_tx, NQ * b + 2 * o + 2)
                        load(b, o + 2, u)
                        store(b, o, u)
                for u in range(2):
                    store(b, NO - 2 + u, u)

            def output(b):
                for h in range(2):
                    sp.wait_ge(s_out, 2 * b + h + 1)
                    t0 = NT // 2 * h
                    sp.dma_start(out[b].rearrange("(t p) d -> p t d", p=P)[:, t0:t0 + NT // 2, :],
                                 x_all[:, b * NT + t0:b * NT + t0 + NT // 2, :]).then_inc(d_out, 16)

            for ph, b in phases:
                if ph == "E":
                    experts(b)
                if ph == "C":
                    output(b)
            sp.wait_ge(d_out, 16 * 2 * NB)

        @block.gpsimd
        def _(pool):
            g = nc.gpsimd
            g.memset(ident[:, :], 0.0)
            g.memset(ones[:, :], 1.0)
            g.memset(ident_bf[:, :], 0.0)
            g.memset(ones_bf[:, :], 1.0)
            g.memset(before_bf[:, :], 1.0)
            g.memset(lower_g[:, :, :], 1.0).then_inc(s_const, 1)
            pool.wait_ge(s_const, 1)
            g.affine_select(out=ident[:, :], in_=ident[:, :], compare_op=ALU.not_equal, fill=1.0, base=0,
                            pattern=[[-1, P]], channel_multiplier=1)
            g.affine_select(out=ident_bf[:, :], in_=ident_bf[:, :], compare_op=ALU.not_equal, fill=1.0, base=0,
                            pattern=[[-1, P]], channel_multiplier=1)
            g.affine_select(out=before_bf[:, :], in_=before_bf[:, :], compare_op=ALU.is_gt, fill=0.0, base=0,
                            pattern=[[1, P]], channel_multiplier=-1)
            g.affine_select(out=lower_g[:, :, :], in_=lower_g[:, :, :], compare_op=ALU.is_gt, fill=0.0, base=0,
                            pattern=[[1, NG], [-1, NG]], channel_multiplier=0)
            g.iota(iota_i[:, :], pattern=[[1, 1]], base=0, channel_multiplier=1).then_inc(s_const, 1)

            def scatter(b):
                pool.wait_ge(s_x1r, b + 1)
                pool.wait_ge(s_slot, b + 1)
                if b < 2:
                    pool.wait_ge(s_fill[b], 16)
                else:
                    for r in range(2):
                        pool.wait_ge(d_ld[r], 16 * (NQ // 4) * (b - 1))
                for t in range(NT):
                    for k in range(K):
                        c = t * K + k
                        g.indirect_dma_start(
                            out=xs[b % 2], out_offset=bass.IndirectOffsetOnAxis(ap=slots[:, b, c:c + 1], axis=0),
                            in_=x1r[:, b % 2 * NT + t, :], in_offset=None).then_inc(d_scat[b], 16)

            def gather(b):
                for r in range(2):
                    pool.wait_ge(d_st[r], 16 * (NQ // 4) * (b + 1))
                if b:
                    pool.wait_ge(s_acc, NT * K * b)
                for t in range(NT):
                    for k in range(K):
                        c = t * K + k
                        g.indirect_dma_start(
                            out=gbuf[:, t, k, :], out_offset=None, in_=os[b % 2],
                            in_offset=bass.IndirectOffsetOnAxis(ap=slots[:, b, c:c + 1], axis=0)
                        ).then_inc(d_gat[b][t // (NT // 2)], 16)

            scatter(0)
            scatter(1)
            gather(0)
            scatter(2)
            gather(1)
            scatter(3)
            gather(2)
            gather(3)

        @block.tensor
        def _(pe):
            mm = nc.tensor.matmul
            tr = nc.tensor.transpose

            def dense(b):
                if b == 0:
                    pe.wait_ge(s_const, 2)
                if e_before_a(b):
                    pe.wait_ge(s_eo, NQ * e_before_a(b))
                    pe.wait_ge(s_ht, NQ * e_before_a(b))
                    pe.wait_ge(s_eh, NQ * e_before_a(b))
                elif b:
                    pe.wait_ge(s_res, 2 * b)
                pe.wait_ge(d_x[b], 16)
                for t in range(NT):
                    ins = tr(gu_flat[:, T + t * P:T + (t + 1) * P], x_all[:, b * NT + t, :], ident[:, :])
                ins.then_inc(p_xT, 1)
                pe.wait_ge(s_yr, b + 1)
                for t in range(NT):
                    ins = tr(gu_flat[:, t * P:(t + 1) * P], work_b[:, t * P:(t + 1) * P], ident[:, :])
                ins.then_inc(p_yT, 1)
                pe.wait_ge(s_sq2, b + 1)
                for t in range(NT):
                    ins = mm(MI[:, t:t + 1], work_a[:, t * P:(t + 1) * P], ones[:, 0:1], start=True, stop=True)
                ins.then_inc(p_ss2, 1)
                pe.wait_ge(s_diag, b + 1)
                pe.wait_ge(s_xT, b + 1)
                for c in range(2):
                    ins = mm(GU[:, 2 + c, :], ones[:, :], work_b[:, c * 512:(c + 1) * 512], start=True, stop=True)
                ins.then_inc(p_rs, 1)
                pe.wait_ge(s_z, b + 1)
                if b == 0:
                    pe.wait_ge(s_mlpw, 48)
                    pe.wait_ge(s_par, 32)
                for c in range(2):
                    z = zT[:, c * 512:(c + 1) * 512]
                    for m in range(NM):
                        n = c * NM + m
                        if n >= 2:
                            pe.wait_ge(s_h, 2 * NM * b + n - 1)
                        mm(GU[:, 2 * (n % 2), :], wgate_sb[:, m * P:(m + 1) * P], z, start=True, stop=True)
                        mm(GU[:, 2 * (n % 2) + 1, :], wup_sb[:, m * P:(m + 1) * P], z, start=True,
                           stop=True).then_inc(p_gu, 1)
                    dst = XT if c == 0 else HT
                    mm(dst[:, :], ones[0:1, :], bdown_sb[:, :].unsqueeze(1).to_broadcast([1, 4, P]),
                       start=True, stop=False, skip_group_check=True)
                    for t in range(4):
                        tok = slice((4 * c + t) * P, (4 * c + t + 1) * P)
                        mm(dst[:, t * P:(t + 1) * P], x2T[:, tok], ident[:, :], start=False, stop=False,
                           skip_group_check=True)
                    for m in range(NM):
                        pe.wait_ge(s_h, 2 * NM * b + c * NM + m + 1)
                        for t in range(4):
                            ins = mm(dst[:, t * P:(t + 1) * P], h_sb[:, m, t * P:(t + 1) * P], wdown_sb[:, m, :],
                                     start=False, stop=(m == NM - 1), skip_group_check=True)
                    ins.then_inc(p_dn, 1)
                pe.wait_ge(s_x1r, b + 1)
                for t in range(NT):
                    ins = tr(gu_flat[:, t * P:(t + 1) * P], x1r[:, b % 2 * NT + t, :], ident[:, :])
                ins.then_inc(p_x1, 1)
                pe.wait_ge(s_x1T, b + 1)
                if b == 0:
                    pe.wait_ge(s_shw, 64)
                for t in range(NT):
                    ins = mm(MI[:, t * E:(t + 1) * E], zT[:, t * P:(t + 1) * P], gatew_sb[:, :], start=True, stop=True)
                ins.then_inc(p_lg, 1)

                def shared(n):
                    c, j = n // SJ, n % SJ
                    if n >= 2:
                        pe.wait_ge(s_sh, 2 * SJ * b + n - 1)
                    z = zT[:, c * 512:(c + 1) * 512]
                    mm(GU[0:I, 2 * (n % 2), :], sgu_sb[:, 0, j, :], z, start=True, stop=True)
                    mm(GU[0:I, 2 * (n % 2) + 1, :], sgu_sb[:, 1, j, :], z, start=True, stop=True).then_inc(p_sh, 1)

                shared(0)
                shared(1)
                pe.wait_ge(s_sel, b + 1)
                mm(OT[:, :], before_bf[:, :], sel[:, :, :].rearrange("p t e -> p (t e)"), start=True, stop=False,
                   skip_group_check=True)
                for t in range(NT - 1):
                    n = NT - 1 - t
                    mm(OT[:, (t + 1) * E:], ones_bf[:, :], sel[:, t, :].unsqueeze(1).to_broadcast([P, n, E]),
                       start=False, stop=(t == NT - 2), skip_group_check=True)
                for t in range(NT):
                    ins = mm(MI[:, 0:E], ones_bf[:, :], sel[:, t, :], start=(t == 0), stop=(t == NT - 1))
                ins.then_inc(p_rank, 1)
                pe.wait_ge(s_ecol, b + 1)
                mm(MI[0:1, P:2 * P], eid_bf[:, :], ident_bf[:, :], start=True, stop=True).then_inc(p_erow, 1)
                shared(2)
                shared(3)
                for c in range(2):
                    dst = XT if c == 0 else HT
                    pe.wait_ge(s_sh, 2 * SJ * b + SJ * (c + 1))
                    for t in range(4):
                        tok = slice((4 * c + t) * P, (4 * c + t + 1) * P)
                        for j in range(SJ):
                            ins = mm(dst[:, t * P:(t + 1) * P], hs[0:I, j, tok], sd_sb[:, j, :], start=(j == 0),
                                     stop=(j == SJ - 1))
                    ins.then_inc(p_sd, 1)

            def expert_ids(b, q):
                return [pe.value_load(eid[0:1, b % 2, bass.ds(q * QUAD + i, 1)], min_val=0, max_val=E - 1)
                        for i in range(QUAD)]

            def transpose_x(b, q, u):
                half = (u // 2) % 2
                if u % 2 == 0:
                    pe.wait_ge(d_ld[half], 16 * ((NQ // 4) * b + (q - u) // 4 + u // 4 + 1) if isinstance(q, int)
                               else 16 * ((NQ // 4) * b + 1) + (q - u) * 4 + 16 * (u // 4))
                if has(b, q, 1):
                    pe.wait_ge(s_xg, NQ * b + q)
                for i in range(QUAD):
                    ins = tr(XT[:, i * P:(i + 1) * P], xl[:, half, (u % 2) * QUAD + i, :], ident[:, :])
                ins.then_inc(p_tx, 1)

            def gate_up(b, q, u):
                ids = expert_ids(b, q)
                pe.wait_ge(s_xg, NQ * b + q + 1)
                if has(b, q, 2):
                    pe.wait_ge(s_eh, NQ * b + q - 1)
                for i in range(QUAD):
                    r = u % 2
                    ins = mm(GU[:, 2 * r + i // 2, (i % 2) * 2 * I:(i % 2 + 1) * 2 * I], xg[:, r, i * P:(i + 1) * P],
                             wgu_sb[:, bass.ds(ids[i], 1), :].rearrange("p a c -> p (a c)"), start=True, stop=True)
                ins.then_inc(p_eg, 1)

            def transpose_h(b, q, u):
                pe.wait_ge(s_eh, NQ * b + q + 1)
                if has(b, q, 1):
                    pe.wait_ge(s_ht, NQ * b + q)
                for i in range(QUAD):
                    ins = tr(HT[0:I, i * P:(i + 1) * P], eh[:, u % 2, i * I:(i + 1) * I], ident[:, :])
                ins.then_inc(p_th, 1)

            def down(b, q, u):
                ids = expert_ids(b, q)
                pe.wait_ge(s_ht, NQ * b + q + 1)
                if has(b, q, 1):
                    pe.wait_ge(s_eo, NQ * b + q)
                for i in range(QUAD):
                    ins = mm(OT[:, i * P:(i + 1) * P], hT[0:I, u % 2, i * P:(i + 1) * P],
                             wd_sb[:, bass.ds(ids[i], 1), :].rearrange("p a c -> p (a c)"), start=True, stop=True)
                ins.then_inc(p_eo, 1)

            def step(b, q, u):
                if not (isinstance(q, int) and q + 2 >= NQ):
                    transpose_x(b, q + 2, u + 2)
                if not (isinstance(q, int) and q + 1 >= NQ):
                    gate_up(b, q + 1, u + 1)
                transpose_h(b, q, u)
                if not (isinstance(q, int) and q == 0):
                    down(b, q - 1, u + 1)

            def experts(b):
                pe.wait_ge(s_res, 2 * a_before_e(b))
                pe.wait_ge(s_eid, b + 1)
                if b == 0:
                    pe.wait_ge(s_expw, 32)
                transpose_x(b, 0, 0)
                transpose_x(b, 1, 1)
                gate_up(b, 0, 0)
                quads(step)(pe, b)
                down(b, NQ - 1, NQ - 1)

            for ph, b in phases:
                if ph == "A":
                    dense(b)
                if ph == "E":
                    experts(b)

        @block.scalar
        def _(act):
            f = nc.scalar.activation

            act.wait_ge(s_par, 32)
            f(tanh_a[:, :], vec[:, V_A:V_A + 1], ACT.Tanh).then_inc(s_cact, 1)
            act.wait_ge(s_cdve, 1)

            def dense(b):
                if b:
                    act.wait_ge(s_wk, b)
                act.wait_ge(d_x[b], 16)
                f(work_a[:, :], x_all[:, b * NT:(b + 1) * NT, :].rearrange("p t d -> p (t d)"),
                  ACT.Square).then_inc(s_sqx, 1)
                act.wait_ge(s_ssx, b + 1)
                f(rs[:, 0, :], ss[:, 0, :], ACT.Sqrt, bias=eps[:, 0:1], scale=1.0 / P).then_inc(s_sdx, 1)
                act.wait_ge(p_xT, b + 1)
                f(x2T[:, :], gu_flat[:, T:2 * T], ACT.Identity, bias=vec[:, V_CB:V_CB + 1]).then_inc(s_xT, 1)
                act.wait_ge(p_yT, b + 1)
                f(yT[:, 1:T + 1], gu_flat[:, 0:T], ACT.Identity, scale=vec[:, V_NORM:V_NORM + 1]).then_inc(s_yT, 1)
                act.wait_ge(s_x2, b + 1)
                f(work_a[:, :], x2T[:, :], ACT.Square).then_inc(s_sq2, 1)
                act.wait_ge(p_ss2, b + 1)
                f(rs[:, 1, :], MI[:, 0:NT], ACT.Sqrt, bias=eps[:, 0:1], scale=1.0 / P).then_inc(s_sd2, 1)
                for n in range(2 * NM):
                    m = n % NM
                    act.wait_ge(p_gu, 2 * NM * b + n + 1)
                    if n >= 2:
                        act.wait_ge(s_h, 2 * NM * b + n - 1)
                    f(gbuf2[:, n % 2, :], GU[:, 2 * (n % 2), :], ACT.Silu,
                      bias=vec[:, V_BG + m:V_BG + m + 1]).then_inc(s_sil, 1)
                act.wait_ge(s_mv, b + 1)
                f(rs[:, 2, :], mv[:, :, 1], ACT.Sqrt, bias=eps[:, 1:2]).then_inc(s_sd3, 1)
                act.wait_ge(p_x1, b + 1)
                f(zT[:, :], gu_flat[:, 0:T], ACT.Copy).then_inc(s_x1T, 1)
                act.wait_ge(p_lg, b + 1)
                f(score, MI[:, :].rearrange("p (t e) -> p t e", e=E), ACT.Sigmoid).then_inc(s_sc, 1)
                for n in range(2 * SJ):
                    act.wait_ge(p_sh, 2 * SJ * b + n + 1)
                    if n >= 2:
                        act.wait_ge(s_sh, 2 * SJ * b + n - 1)
                    f(gbuf2[0:I, n % 2, :], GU[0:I, 2 * (n % 2), :], ACT.Silu).then_inc(s_ssil, 1)

            def take_x(b, q, u):
                act.wait_ge(p_tx, NQ * b + q + 1)
                if has(b, q, 2):
                    act.wait_ge(p_eg, NQ * b + q - 1)
                f(xg[:, u % 2, :], XT[:, :], ACT.Copy).then_inc(s_xg, 1)

            def silu(b, q, u):
                r = u % 2
                act.wait_ge(p_eg, NQ * b + q + 1)
                if has(b, q, 2):
                    act.wait_ge(s_eh, NQ * b + q - 1)
                f(eg[:, r, :].rearrange("p (a t c) -> p a t c", a=2, t=2),
                  GU[:, 2 * r:2 * r + 2, 0:4 * I].rearrange("p a (t c) -> p a t c", c=2 * I)[:, :, :, 0:I],
                  ACT.Silu).then_inc(s_eg, 1)

            def take_out(b, q, u):
                half = (u // 2) % 2
                act.wait_ge(p_eo, NQ * b + q + 1)
                first = isinstance(q, int) and q < UN
                if u % 2 == 0 and not (first and b == 0):
                    if isinstance(q, int):
                        act.wait_ge(d_st[half], 16 * ((NQ // 4) * b + q // 4))
                    else:
                        act.wait_ge(d_st[half], 16 * (NQ // 4) * b + (q - u) * 4 + 16 * (u // 4))
                f(ol[:, half, (u % 2) * QUAD:(u % 2 + 1) * QUAD, :].rearrange("p t d -> p (t d)"), OT[:, :],
                  ACT.Copy).then_inc(s_eo, 1)

            def step(b, q, u):
                if not (isinstance(q, int) and q + 2 >= NQ):
                    take_x(b, q + 2, u + 2)
                if not (isinstance(q, int) and q + 1 >= NQ):
                    silu(b, q + 1, u + 1)
                if not (isinstance(q, int) and q == 0):
                    take_out(b, q - 1, (u - 1) if isinstance(q, int) else u + UN - 1)

            def experts(b):
                act.wait_ge(s_res, 2 * a_before_e(b))
                nc.scalar.preload_act_table(ACT.Silu)
                take_x(b, 0, 0)
                take_x(b, 1, 1)
                silu(b, 0, 0)
                quads(step)(act, b)
                take_out(b, NQ - 1, NQ - 1)

            def combine(b):
                for h in range(2):
                    act.wait_ge(s_cmv, 2 * b + h + 1)
                    f(csd[:, 0, :], cmv[:, :, 1], ACT.Sqrt, bias=eps[:, 1:2]).then_inc(s_csd, 1)

            for ph, b in phases:
                {"A": dense, "E": experts, "C": combine}[ph](b)

        @block.vector
        def _(dve):
            v = nc.vector
            done = [0]

            def then(ins):
                done[0] += 1
                ins.then_inc(dv, 1)
                dve.wait_ge(dv, done[0])

            def bc(ap, *shape):
                return ap.to_broadcast(list(shape))

            v.memset(gbuf[:, 0, :, :], 0.0).then_inc(s_zero, 1)
            v.memset(yT[:, :], 0.0)
            v.memset(eps[:, 0:1], RMS_EPS)
            v.memset(eps[:, 1:2], LN_EPS).then_inc(s_cdve, 1)
            dve.wait_ge(s_const, 2)
            then(v.tensor_copy(iota_f[:, :], iota_i[:, :]))
            dve.wait_ge(s_cact, 1)

            def vc(c):
                return vec[:, c:c + 1]

            def dense(b):
                xb = x_all[:, b * NT:(b + 1) * NT, :]
                wa = work_a[:, :].rearrange("p (t d) -> p t d", d=P)
                wb = work_b[:, :].rearrange("p (t d) -> p t d", d=P)
                dve.wait_ge(s_sqx, b + 1)
                v.tensor_reduce(ss[:, 0, :], wa, AX_X, ALU.add).then_inc(s_ssx, 1)
                dve.wait_ge(s_sdx, b + 1)
                then(v.reciprocal(ss[:, 0, :], rs[:, 0, :]))
                v.tensor_tensor(wb, xb, bc(ss[:, 0, :].unsqueeze(2), P, NT, P), ALU.mult).then_inc(s_yr, 1)
                dve.wait_ge(s_yT, b + 1)
                v.tensor_tensor_scan(work_a[:, :], bc(tanh_a[:, 0:1], P, T), yT[:, 1:T + 1], 0.0, ALU.mult, ALU.add)
                dve.wait_ge(s_xT, b + 1)
                for k in range(3):
                    then(v.scalar_tensor_tensor(out=x2T[:, :], in0=yT[:, k:k + T], scalar=vc(V_CW + k),
                                                in1=x2T[:, :], op0=ALU.mult, op1=ALU.add))
                v.scalar_tensor_tensor(out=x2T[:, :], in0=work_a[:, :], scalar=vc(V_B), in1=x2T[:, :],
                                       op0=ALU.mult, op1=ALU.add).then_inc(s_x2, 1)
                dve.wait_ge(s_sd2, b + 1)
                then(v.reciprocal(ss[:, 1, :], rs[:, 1, :]))
                v.tensor_tensor(wb, bc(ident[:, :].unsqueeze(1), P, NT, P), bc(ss[:, 1, :].unsqueeze(2), P, NT, P),
                                ALU.mult).then_inc(s_diag, 1)
                dve.wait_ge(p_rs, b + 1)
                dve.wait_ge(s_x2, b + 1)
                v.scalar_tensor_tensor(out=zT[:, :], in0=x2T[:, :], scalar=vc(V_MN), in1=gu_flat[:, T:2 * T],
                                       op0=ALU.mult, op1=ALU.mult).then_inc(s_z, 1)
                for c in range(2):
                    for m in range(NM):
                        n = c * NM + m
                        dve.wait_ge(s_sil, 2 * NM * b + n + 1)
                        if c and m == 0:
                            dve.wait_ge(p_dn, 2 * b + 1)
                        v.scalar_tensor_tensor(out=h_sb[:, m, :], in0=GU[:, 2 * (n % 2) + 1, :], scalar=vc(V_BU + m),
                                               in1=gbuf2[:, n % 2, :], op0=ALU.add, op1=ALU.mult).then_inc(s_h, 1)
                for c in range(2):
                    dve.wait_ge(p_dn, 2 * b + c + 1)
                    v.tensor_tensor(wb[:, 4 * c:4 * c + 4, :], (XT if c == 0 else HT)[:, :].rearrange(
                        "p (t d) -> p t d", d=P), xb[:, 4 * c:4 * c + 4, :], ALU.add).then_inc(s_v, 1)
                dve.wait_ge(s_v, 2 * b + 2)
                for t in range(NT):
                    last = v.bn_stats(stats[:, t, :], wb[:, t, :])
                then(last)
                for t in range(NT):
                    last = v.bn_aggr(mv[:, t, :], stats[:, t, :])
                last.then_inc(s_mv, 1)
                dve.wait_ge(s_sd3, b + 1)
                then(v.reciprocal(ss[:, 2, :], rs[:, 2, :]))
                if b >= 2:
                    dve.wait_ge(d_scat[b - 2], 16 * NT * K)
                for t in range(NT):
                    last = v.tensor_scalar(x1r[:, b % 2 * NT + t, :], wb[:, t, :], mv[:, t, 0:1], ss[:, 2, t:t + 1],
                                           ALU.subtract, ALU.mult)
                last.then_inc(s_x1r, 1)
                route(b)
                shared(b)
                weights(b)

            def route(b):
                ch4 = work_b[:, 512:1024].rearrange("p (g e) -> p g e", e=EG)
                ta4 = work_a[:, 0:512].rearrange("p (g e) -> p g e", e=EG)
                tb4 = work_a[:, 512:1024].rearrange("p (g e) -> p g e", e=EG)
                n = NT * NG
                m1, m2, ties, gs = (small[:, i, :] for i in range(4))
                dve.wait_ge(s_sc, b + 1)
                then(v.tensor_tensor(choice, score, bc(gbias_sb[:, :].unsqueeze(1), P, NT, E), ALU.add))
                then(v.tensor_reduce(m1, ch4, AX_X, ALU.max))
                then(v.tensor_tensor(ta4, ch4, bc(m1.unsqueeze(2), P, n, EG), ALU.is_equal))
                v.tensor_reduce(ties, ta4, AX_X, ALU.add)
                then(v.scalar_tensor_tensor(out=tb4, in0=ta4, scalar=-BIG, in1=ch4, op0=ALU.mult, op1=ALU.add))
                v.tensor_reduce(m2, tb4, AX_X, ALU.max)
                then(v.tensor_scalar(ties, ties, 1.5, -BIG, ALU.is_lt, ALU.mult))
                then(v.tensor_tensor(ties, ties, m1, ALU.add))
                then(v.tensor_tensor(m2, m2, ties, ALU.max))
                then(v.tensor_tensor(gs, m1, m2, ALU.add))
                g3 = gs.rearrange("p (t g) -> p t g", g=NG)
                mine = bc(g3.unsqueeze(3), P, NT, NG, NG)
                other = bc(g3.unsqueeze(2), P, NT, NG, NG)
                ta5 = work_a[:, 0:512].rearrange("p (t g e) -> p t g e", g=NG, e=NG)
                tb5 = work_a[:, 512:1024].rearrange("p (t g e) -> p t g e", g=NG, e=NG)
                then(v.tensor_tensor(ta5, other, mine, ALU.is_equal))
                v.tensor_tensor(tb5, other, mine, ALU.is_gt)
                then(v.tensor_tensor(ta5, ta5, bc(lower_g[:, :, :].unsqueeze(1), P, NT, NG, NG), ALU.mult))
                then(v.tensor_tensor(ta4, ta4, tb4, ALU.add))
                then(v.tensor_reduce(m1, ta4, AX_X, ALU.add))
                then(v.tensor_scalar(m2, m1, TOPG - 0.5, None, ALU.is_lt))
                then(v.tensor_tensor(ch4, ch4, bc(m2.unsqueeze(2), P, n, EG), ALU.mult))
                then(v.tensor_scalar(choice, choice, 0.0, None, ALU.add))
                for t in range(NT):
                    last = v.max(top[:, t, :], choice[:, t, :])
                then(last)
                for t in range(NT):
                    last = v.match_replace(out=tab_a[:, t, :], in_to_replace=top[:, t, :], in_values=choice[:, t, :],
                                           imm_value=GONE)
                then(last)
                v.tensor_scalar(sel[:, :, :], tab_a, GONE, None, ALU.is_equal).then_inc(s_sel, 1)
                dve.wait_ge(s_sel, b + 1)
                then(v.tensor_tensor(tab_b, sel[:, :, :], score, ALU.mult))
                then(v.tensor_reduce(wsum[:, 0, :], tab_b, AX_X, ALU.add))
                then(v.tensor_scalar(wsum[:, 0, :], wsum[:, 0, :], 1e-20, None, ALU.add))
                then(v.reciprocal(wsum[:, 1, :], wsum[:, 0, :]))
                then(v.tensor_scalar(wsum[:, 1, :], wsum[:, 1, :], ROUTED_SCALE, None, ALU.mult))
                v.tensor_tensor(rw[:, :, :], tab_b, bc(wsum[:, 1, :].unsqueeze(2), P, NT, E), ALU.mult)
                dve.wait_ge(p_rank, b + 1)
                then(v.tensor_scalar(cnt_i[:, 0, :], MI[:, 0:E], float(P - 1), None, ALU.add))
                then(v.tensor_scalar(cnt_i[:, 1, :], cnt_i[:, 0, :], P.bit_length() - 1, None,
                                     ALU.logical_shift_right))
                then(v.tensor_copy(tiles[:, 0, :], cnt_i[:, 1, :]))
                then(v.tensor_tensor_scan(tiles[:, 1, :], bc(ones[:, 0:1], P, E), tiles[:, 0, :], 0.0,
                                          ALU.mult, ALU.add))
                then(v.tensor_tensor(tiles[:, 2, :], tiles[:, 1, :], tiles[:, 0, :], ALU.subtract))
                then(v.tensor_scalar(tiles[:, 2, :], tiles[:, 2, :], float(P), 1.0, ALU.mult, ALU.add))
                then(v.tensor_tensor(key[:, :, :], OT[:, :].rearrange("p (t e) -> p t e", e=E),
                                     bc(tiles[:, 2, :].unsqueeze(1), P, NT, E), ALU.add))
                then(v.tensor_tensor(key[:, :, :], key[:, :, :], sel[:, :, :], ALU.mult))
                for t in range(NT):
                    last = v.max(keys[:, t, :], key[:, t, :])
                then(last)
                v.tensor_scalar(slots[:, b, :], keys[:, :, :].rearrange("p t k -> p (t k)"), -1.0, None,
                                ALU.add).then_inc(s_slot, 1)
                then(v.tensor_scalar(small[:, 5, :], tiles[:, 1, :], iota_f[:, 0:1], None, ALU.is_le))
                then(v.tensor_reduce(eid_col[:, 0:1], small[:, 5, :], AX_X, ALU.add))
                v.tensor_scalar(eid_bf[:, :], eid_col[:, 0:1], float(E - 1), None, ALU.min).then_inc(s_ecol, 1)
                dve.wait_ge(p_erow, b + 1)
                if b >= 2:
                    dve.wait_ge(p_eo, NQ * (b - 1))
                v.tensor_copy(eid[0:1, b % 2, :], MI[0:1, P:2 * P]).then_inc(s_eid, 1)

            def shared(b):
                for n in range(2 * SJ):
                    c, j = n // SJ, n % SJ
                    dve.wait_ge(s_ssil, 2 * SJ * b + n + 1)
                    v.tensor_tensor(hs[0:I, j, c * 512:(c + 1) * 512], GU[0:I, 2 * (n % 2) + 1, :],
                                    gbuf2[0:I, n % 2, :], ALU.mult).then_inc(s_sh, 1)
                for c in range(2):
                    dve.wait_ge(p_sd, 2 * b + c + 1)
                    t0 = b * NT + 4 * c
                    r0 = b % 2 * NT + 4 * c
                    v.tensor_tensor(x_all[:, t0:t0 + 4, :], (XT if c == 0 else HT)[:, :].rearrange(
                        "p (t d) -> p t d", d=P), x1r[:, r0:r0 + 4, :], ALU.add).then_inc(s_res, 1)

            def weights(b):
                for t in range(NT):
                    then(v.tensor_tensor(tab_a, bc(key[:, t, :].unsqueeze(1), P, K, E),
                                         bc(keys[:, t, :].unsqueeze(2), P, K, E), ALU.is_equal))
                    then(v.tensor_tensor(tab_a, tab_a, bc(rw[:, t, :].unsqueeze(1), P, K, E), ALU.mult))
                    last = v.tensor_reduce(wk[:, b, t * K:(t + 1) * K], tab_a, AX_X, ALU.add)
                    if t < NT - 1:
                        then(last)
                last.then_inc(s_wk, 1)

            def mul_h(b, q, u):
                r = u % 2
                dve.wait_ge(s_eg, NQ * b + q + 1)
                if has(b, q, 2):
                    dve.wait_ge(p_th, NQ * b + q - 1)
                v.tensor_tensor(
                    eh[:, r, :].rearrange("p (a t c) -> p a t c", a=2, t=2),
                    GU[:, 2 * r:2 * r + 2, 0:4 * I].rearrange("p a (t c) -> p a t c", c=2 * I)[:, :, :, I:2 * I],
                    eg[:, r, :].rearrange("p (a t c) -> p a t c", a=2, t=2), ALU.mult).then_inc(s_eh, 1)

            def take_h(b, q, u):
                dve.wait_ge(p_th, NQ * b + q + 1)
                if has(b, q, 2):
                    dve.wait_ge(p_eo, NQ * b + q - 1)
                v.tensor_copy(hT[0:I, u % 2, :], HT[0:I, :]).then_inc(s_ht, 1)

            def step(b, q, u):
                if not (isinstance(q, int) and q + 1 >= NQ):
                    mul_h(b, q + 1, u + 1)
                take_h(b, q, u)

            def experts(b):
                mul_h(b, 0, 0)
                quads(step)(dve, b)

            def combine(b):
                hn = NT // 2
                if b == 0:
                    dve.wait_ge(s_wk, 1)
                for h in range(2):
                    base = NT * K * b + hn * K * h
                    t0 = h * hn
                    dve.wait_ge(d_gat[b][h], 16 * hn * K)
                    dve.wait_ge(s_res, 2 * b + h + 1)
                    with dve.Fori(0, K) as k:
                        for t in range(hn):
                            rowap = x_all[:, b * NT + t0 + t, :]
                            dve.wait_ge(s_acc, base + k * hn + t - hn + 1 if base else k * hn + t + 1 - hn) if base else None
                            v.scalar_tensor_tensor(
                                out=rowap, in0=gbuf[:, t0 + t, bass.ds(k, 1), :].rearrange("p a d -> p (a d)"),
                                scalar=wk[:, b, bass.ds(k + (t0 + t) * K, 1)], in1=rowap,
                                op0=ALU.mult, op1=ALU.add).then_inc(s_acc, 1)
                            if not base:
                                dve.wait_ge(s_acc, k * hn + t + 1)
                    dve.wait_ge(s_acc, base + hn * K)
                    for t in range(hn):
                        last = v.bn_stats(cst[:, t, :], x_all[:, b * NT + t0 + t, :])
                    then(last)
                    for t in range(hn):
                        last = v.bn_aggr(cmv[:, t, :], cst[:, t, :])
                    last.then_inc(s_cmv, 1)
                    dve.wait_ge(s_csd, 2 * b + h + 1)
                    then(v.reciprocal(csd[:, 1, :], csd[:, 0, :]))
                    for t in range(hn):
                        rowap = x_all[:, b * NT + t0 + t, :]
                        last = v.tensor_scalar(rowap, rowap, cmv[:, t, 0:1], csd[:, 1, t:t + 1],
                                               ALU.subtract, ALU.mult)
                    last.then_inc(s_out, 1)

            for ph, b in phases:
                {"A": dense, "E": experts, "C": combine}[ph](b)


def kernel(**inputs):
    import numpy as np
    import concourse.bacc as bacc
    from concourse.bass_utils import run_bass_kernel_spmd as run

    g = {k[3:]: np.asarray(a) for k, a in inputs.items()}
    a = lambda n: g["attn_" + n]
    f = lambda n: g["ffn_" + n]
    cols = [a("norm_w"), *a("conv_w")[:, 0, :].T, a("conv_b"), a("a"), a("b"), a("mlp_norm_w"),
            *a("b_gate").reshape(NM, P), *a("b_up").reshape(NM, P)]
    ins = {
        "x": a("x"),
        "vecs": np.stack(cols, axis=1),
        "w_gate": a("w_gate"),
        "w_up": a("w_up"),
        "w_down": a("w_down"),
        "b_down": a("b_down").reshape(1, P),
        "gate_wT": f("gate_w").T,
        "gate_bias": f("gate_bias"),
        "wgu": np.concatenate([f("Wg"), f("Wu")], axis=1).transpose(2, 0, 1),
        "wd": f("Wd").transpose(2, 0, 1),
        "sgu": np.stack([f("Sg"), f("Su")]).reshape(2, SJ, I, P).transpose(3, 0, 1, 2),
        "sd": f("Sd").T.reshape(SJ, I, P).transpose(1, 0, 2),
    }
    ins = {n: np.ascontiguousarray(v) for n, v in ins.items()}
    nc = bacc.Bacc("TRN2", target_bir_lowering=False, num_devices=1)
    aps = {n: nc.dram_tensor(n + "_dram", v.shape, mybir.dt.from_np(v.dtype), kind="ExternalInput").ap()
           for n, v in ins.items()}
    out = nc.dram_tensor("out_dram", (NB, T, P), F32, kind="ExternalOutput").ap()
    xs = [nc.dram_tensor(f"xs{r}_dram", (SLOTS, P), F32, kind="Internal").ap() for r in range(2)]
    os = [nc.dram_tensor(f"os{r}_dram", (SLOTS, P), F32, kind="Internal").ap() for r in range(2)]
    build(nc, out=out, xs=xs, os=os, **aps)
    r = run(nc, [{n + "_dram": v for n, v in ins.items()}], core_ids=[0])
    return r.results[0]["out_dram"]
```

```python
from contextlib import ExitStack

import concourse.bass as bass
from concourse import mybir

F32 = mybir.dt.float32
BF16 = mybir.dt.bfloat16
I32 = mybir.dt.int32
U32 = mybir.dt.uint32
ALU = mybir.AluOpType
ACT = mybir.ActivationFunctionType
AX_X = mybir.AxisListType.X

P = 128
NB = 4
T = 1024
NT = NB * T // P
C = 512
CT = C // P
NC = NB * T // C
SC = T // C
HID = 512
NM = HID // P
E = 64
I = 88
K = 8
NG = 8
EG = E // NG
TOPG = 4
SJ = 2
ROUTED_SCALE = 2.5
RMS_EPS = 1e-6
LN_EPS = 1e-5
BIG = 1e30
GONE = -3e38

BATCHES = (2, 3, 3)
NBAT = len(BATCHES)
FIRST = [sum(BATCHES[:b]) for b in range(NBAT + 1)]
ET = [n * CT * K + E for n in BATCHES]
ET0 = [sum(ET[:b]) for b in range(NBAT + 1)]
QUAD = 4
NQ = ET0[-1] // QUAD
Q0 = [e // QUAD for e in ET0]
UN = 4
SUM_AT = (16, 19, 22, 25)
WT = NT // SUM_AT[0]

FILL_PARTS = 4

V_NORM, V_CW, V_CB, V_A, V_B, V_MN, V_BG, V_BU = 0, 1, 4, 5, 6, 7, 8, 8 + NM
NV = 8 + 2 * NM

M_LG, M_SS, M_YB = 0, 256, 264
H_RANK, H_CNT, H_END, H_START = 0, 256, 257, 320


def batch_of(c):
    return max(b for b in range(NBAT) if FIRST[b] <= c)


def build(nc, x, vecs, w_gate, w_up, w_down, b_down, gate_wT, gate_bias, wgu, wd, sgu, sd, out, xs, os):
    with ExitStack() as ctx:
        def sb(name, shape, dt=F32):
            return ctx.enter_context(nc.sbuf_tensor(name, shape, dt))

        def psum(name, shape, dt=F32):
            return ctx.enter_context(nc.psum_tensor(name, shape, dt))

        def sem(name):
            return ctx.enter_context(nc.semaphore(name))

        wgu_sb = sb("wgu_sb", [P, E * 2 * I])
        wd_sb = sb("wd_sb", [I, E * P])
        mlpw_sb = sb("mlpw_sb", [P, 3 * HID])
        wgate_sb, wup_sb = mlpw_sb[:, 0:HID], mlpw_sb[:, HID:2 * HID]
        wdown_sb = mlpw_sb[:, 2 * HID:].rearrange("p (m d) -> p m d", d=P)
        bdown_sb = sb("bdown_sb", [1, P])
        gatew_sb = sb("gatew_sb", [P, E])
        gbias_sb = sb("gbias_sb", [P, E])
        sgu_sb = sb("sgu_sb", [P, 2, SJ, I])
        sd_sb = sb("sd_sb", [I, SJ, P])
        vec = sb("vec", [P, NV])
        tanh_a = sb("tanh_a", [P, 1])
        eps = sb("eps", [P, 2])
        ident = sb("ident", [P, P])
        ones = sb("ones", [P, P])
        ident_bf = sb("ident_bf", [E, E], BF16)
        ones_bf = sb("ones_bf", [P, P], BF16)
        before_bf = sb("before_bf", [P, P], BF16)
        lower_g = sb("lower_g", [P, NG, NG])
        iota_i = sb("iota_i", [E, max(ET)], I32)
        iota_f = sb("iota_f", [E, max(ET)])

        x_all = sb("x_all", [P, NT, P])
        x1r = sb("x1r", [P, NT, P])
        slots = sb("slots", [P, NT * K], U32)
        keys = sb("keys", [P, NT, K])
        wk = sb("wk", [P, NT * K])
        rw = sb("rw", [P, NT, E])
        key = sb("key", [P, NT, E])
        woff = sb("woff", [1, 2, ET0[-1]], I32)

        sel = sb("sel", [P, 4 * CT, E], BF16)
        ss1 = sb("ss1", [P, NT])
        root = sb("root", [P, 3, NT])
        inv = sb("inv", [P, 3, NT])
        nmean = sb("nmean", [P, NT])
        ycol = sb("ycol", [P, 1])
        stats = sb("stats", [P, CT, 6])
        mv = sb("mv", [P, NT, 2])
        group = sb("group", [P, 4, CT * NG])
        top = sb("top", [P, CT, K])
        wsum = sb("wsum", [P, 2, CT])
        ntile_i = sb("ntile_i", [E, 2], I32)
        ntile_bf = sb("ntile_bf", [E, 1], BF16)
        tile_end = sb("tile_end", [E, 1])
        start = sb("start", [P, E])
        ended = sb("ended", [E, max(ET)], BF16)

        arena = sb("arena", [P, 12288])
        used = [0]

        def cut(*shape):
            size = 1
            for s in shape:
                size *= s
            lo = used[0]
            used[0] += size
            assert used[0] <= 12288
            ap = arena[:, lo:lo + size]
            if len(shape) == 2:
                return ap.rearrange("p (a b) -> p a b", b=shape[1])
            if len(shape) == 4:
                return ap.rearrange("p (a b c d) -> p a b c d", b=shape[1], c=shape[2], d=shape[3])
            return ap

        yr = cut(C)
        yT = cut(2, C + 2)
        scan = cut(2, C)
        x2T = cut(2, C)
        x2q = cut(C)
        diag = cut(C)
        zT = cut(C)
        sil = cut(2, C)
        h_sb = cut(NM, C)
        vr = cut(C)
        x1T = cut(C)
        hs = cut(SJ, C)
        score = cut(CT, E)
        choice = cut(CT, E)
        tab_a = cut(CT, E)
        tab_b = cut(CT, E)
        used[0] = 0
        gbuf = cut(2, CT, K, P)
        xl = cut(4, QUAD * P)
        xg = cut(2, QUAD * P)
        hT = cut(2, QUAD * P)
        egh = mlpw_sb[:, 0:4 * QUAD * I].rearrange("p (a b) -> p a b", b=QUAD * I)
        eg, eh = egh[:, 0:2, :], egh[:, 2:4, :]
        ol = sb("ol", [P, 4, QUAD * P])
        wtab = sb("wtab", [P, K * E])
        cst = sb("cst", [P, CT, 6])
        cmv = sb("cmv", [P, NT, 2])
        csd = sb("csd", [P, 2, NT])

        GU = psum("GU", [P, 4, 512])
        XT = psum("XT", [P, 512])
        HT = psum("HT", [P, 512])
        OT = psum("OT", [P, 512])
        MI = psum("MI", [P, 512])

        s_par = sem("s_par")
        s_mlpw = sem("s_mlpw")
        s_shw = sem("s_shw")
        s_expw = sem("s_expw")
        d_x = [sem(f"d_x{c}") for c in range(NC)]
        s_zero = sem("s_zero")
        d_fill = [sem(f"d_fill{b}") for b in range(NBAT)]
        s_const = sem("s_const")
        s_cdve = sem("s_cdve")
        s_cact = sem("s_cact")
        dv = sem("dv")
        s_ss1 = sem("s_ss1")
        s_root = sem("s_root")
        s_inv = sem("s_inv")
        s_ycol = sem("s_ycol")
        s_yr = sem("s_yr")
        p_xT = sem("p_xT")
        p_yT = sem("p_yT")
        s_xT = sem("s_xT")
        s_yT = sem("s_yT")
        s_x2 = sem("s_x2")
        s_sq2 = sem("s_sq2")
        p_ss2 = sem("p_ss2")
        s_diag = sem("s_diag")
        p_rs = sem("p_rs")
        s_z = sem("s_z")
        p_gu = sem("p_gu")
        s_sil = sem("s_sil")
        s_h = sem("s_h")
        p_dn = sem("p_dn")
        s_v = sem("s_v")
        s_mv = sem("s_mv")
        s_x1r = sem("s_x1r")
        p_x1 = sem("p_x1")
        s_x1T = sem("s_x1T")
        p_lg = sem("p_lg")
        s_sc = sem("s_sc")
        s_sel = sem("s_sel")
        p_rank = sem("p_rank")
        s_key = sem("s_key")
        s_nt = sem("s_nt")
        p_start = sem("p_start")
        s_slot = sem("s_slot")
        s_ended = sem("s_ended")
        p_erow = sem("p_erow")
        s_woff = sem("s_woff")
        p_sh = sem("p_sh")
        s_ssil = sem("s_ssil")
        s_sh = sem("s_sh")
        p_sd = sem("p_sd")
        s_res = sem("s_res")
        s_wk = sem("s_wk")
        d_scat = [sem(f"d_scat{b}") for b in range(NBAT)]
        d_ld = [sem(f"d_ld{r}") for r in range(4)]
        d_st = [sem(f"d_st{r}") for r in range(4)]
        d_gat = [sem(f"d_gat{c}") for c in range(NC)]
        p_tx = sem("p_tx")
        s_xg = sem("s_xg")
        p_eg = sem("p_eg")
        s_eg = sem("s_eg")
        s_eh = sem("s_eh")
        p_th = sem("p_th")
        s_ht = sem("s_ht")
        p_eo = sem("p_eo")
        s_eo = sem("s_eo")
        s_acc = sem("s_acc")
        s_cmv = sem("s_cmv")
        s_csd = sem("s_csd")
        s_out = sem("s_out")
        d_out = sem("d_out")

        xs_t = [a.rearrange("(n p) d -> p n d", p=P) for a in xs]
        os_t = [a.rearrange("(n p) d -> p n d", p=P) for a in os]
        x_t = x.rearrange("b (t p) d -> p (b t) d", p=P)
        out_t = out.rearrange("b (t p) d -> p (b t) d", p=P)

        def tiles(c):
            return range(c * CT, (c + 1) * CT)

        def span(c):
            return slice(c * CT, (c + 1) * CT)

        def ring(c):
            return slice(c % 4 * CT, (c % 4 + 1) * CT)

        def flat(ap):
            return ap.rearrange("p a b -> p (a b)")

        block = ctx.enter_context(nc.Block())

        @block.sync
        def _(sp):
            def load_x(c):
                sp.dma_start(x_all[:, span(c), :], x_t[:, span(c), :]).then_inc(d_x[c], 16)

            def fill(b, parts):
                n = ET[b] * P // parts
                for i in range(parts):
                    sp.dma_start(xs[b][i * n:(i + 1) * n, :].rearrange("(p n c) d -> p n (c d)", p=P, c=K),
                                 flat(ol[:, 0:2, :]).unsqueeze(1).to_broadcast([P, n // P // K, K * P])
                                 ).then_inc(d_fill[b], 16)

            load_x(0)
            load_x(1)
            sp.dma_start(vec[:, :], vecs).then_inc(s_par, 16)
            sp.dma_start(bdown_sb[:, :], b_down).then_inc(s_par, 16)
            sp.dma_start(wgate_sb, w_gate).then_inc(s_mlpw, 16)
            sp.dma_start(wup_sb, w_up).then_inc(s_mlpw, 16)
            sp.dma_start(wdown_sb, w_down.rearrange("(m p) d -> p m d", p=P)).then_inc(s_mlpw, 16)
            for c in range(2, NC):
                load_x(c)
            sp.dma_start(gatew_sb[:, :], gate_wT).then_inc(s_shw, 16)
            sp.dma_start(gbias_sb[:, :], gate_bias.partition_broadcast(P)).then_inc(s_shw, 16)
            sp.dma_start(sgu_sb[:, :, :, :], sgu).then_inc(s_shw, 16)
            sp.dma_start(sd_sb[:, :, :], sd).then_inc(s_shw, 16)
            sp.wait_ge(s_zero, 1)
            fill(0, FILL_PARTS)
            sp.dma_start(wgu_sb[:, :], wgu).then_inc(s_expw, 16)
            sp.dma_start(wd_sb[:, :], wd).then_inc(s_expw, 16)
            for b in range(1, NBAT):
                fill(b, FILL_PARTS)

            def load(b, q, u):
                sp.dma_start(xl[:, u % 4, :].rearrange("p (t d) -> p t d", d=P),
                             xs_t[b][:, bass.ds(q * QUAD, QUAD), :]).then_inc(d_ld[u % 4], 16)

            def store(b, q, u):
                sp.wait_ge(s_eo, q + (Q0[b] + 1))
                sp.dma_start(os_t[b][:, bass.ds(q * QUAD, QUAD), :],
                             ol[:, u % 4, :].rearrange("p (t d) -> p t d", d=P)).then_inc(d_st[u % 4], 16)

            def load_next(q):
                if q + 4 < NQ:
                    b = max(i for i in range(NBAT) if Q0[i] <= q + 4)
                    if q + 4 == Q0[b]:
                        sp.wait_ge(d_scat[b], 16 * BATCHES[b] * CT * K)
                    sp.wait_ge(p_tx, q + 1)
                    load(b, q + 4 - Q0[b], q)

            def store_last(q):
                if q >= 3:
                    b = max(i for i in range(NBAT) if Q0[i] <= q - 3)
                    store(b, q - 3 - Q0[b], q + 1)

            sp.wait_ge(s_res, NC)
            sp.wait_ge(d_scat[0], 16 * BATCHES[0] * CT * K)
            for q in range(4):
                load(0, q, q)
            for b in range(NBAT):
                for q in range(Q0[b], Q0[b] + 4):
                    load_next(q)
                    store_last(q)
                with sp.Fori(1, (Q0[b + 1] - Q0[b]) // 4 - 1) as i:
                    for u in range(4):
                        sp.wait_ge(p_tx, i * 4 + (Q0[b] + u + 1))
                        load(b, i * 4 + (u + 4), u)
                        store(b, i * 4 + (u - 3), u + 1)
                for q in range(Q0[b + 1] - 4, Q0[b + 1]):
                    load_next(q)
                    store_last(q)
            for q in range(NQ, NQ + 3):
                store_last(q)

            for c in range(NC):
                sp.wait_ge(s_out, c + 1)
                sp.dma_start(out_t[:, span(c), :], x_all[:, span(c), :]).then_inc(d_out, 16)
            sp.wait_ge(d_out, 16 * NC)

        @block.gpsimd
        def _(pool):
            g = nc.gpsimd
            g.memset(ident[:, :], 0.0)
            g.memset(ones[:, :], 1.0)
            g.memset(ident_bf[:, :], 0.0)
            g.memset(ones_bf[:, :], 1.0)
            g.memset(before_bf[:, :], 1.0)
            g.memset(lower_g[:, :, :], 1.0).then_inc(s_const, 1)
            pool.wait_ge(s_const, 1)
            g.affine_select(out=ident[:, :], in_=ident[:, :], compare_op=ALU.not_equal, fill=1.0, base=0,
                            pattern=[[-1, P]], channel_multiplier=1)
            g.affine_select(out=ident_bf[:, :], in_=ident_bf[:, :], compare_op=ALU.not_equal, fill=1.0, base=0,
                            pattern=[[-1, E]], channel_multiplier=1)
            g.affine_select(out=before_bf[:, :], in_=before_bf[:, :], compare_op=ALU.is_gt, fill=0.0, base=0,
                            pattern=[[1, P]], channel_multiplier=-1)
            g.affine_select(out=lower_g[:, :, :], in_=lower_g[:, :, :], compare_op=ALU.is_gt, fill=0.0, base=0,
                            pattern=[[1, NG], [-1, NG]], channel_multiplier=0)
            g.iota(iota_i[:, :], pattern=[[1, max(ET)]], base=0, channel_multiplier=0).then_inc(s_const, 1)

            for b in range(NBAT):
                pool.wait_ge(s_x1r, FIRST[b + 1])
                pool.wait_ge(s_slot, b + 1)
                pool.wait_ge(d_fill[b], 16 * FILL_PARTS)
                for t in range(FIRST[b] * CT, FIRST[b + 1] * CT):
                    for k in range(K):
                        c = t * K + k
                        g.indirect_dma_start(
                            out=xs[b], out_offset=bass.IndirectOffsetOnAxis(ap=slots[:, c:c + 1], axis=0),
                            in_=x1r[:, t, :], in_offset=None).then_inc(d_scat[b], 16)
            for c in range(NC):
                b = batch_of(c)
                if c == FIRST[b]:
                    for r in range(4):
                        pool.wait_ge(d_st[r], 4 * Q0[b + 1])
                if c >= 2:
                    pool.wait_ge(s_acc, CT * K * (c - 1))
                for i, t in enumerate(tiles(c)):
                    for k in range(K):
                        g.indirect_dma_start(
                            out=gbuf[:, c % 2, i, k, :], out_offset=None, in_=os[b],
                            in_offset=bass.IndirectOffsetOnAxis(ap=slots[:, t * K + k:t * K + k + 1], axis=0)
                        ).then_inc(d_gat[c], 16)

        @block.tensor
        def _(pe):
            mm = nc.tensor.matmul
            tr = nc.tensor.transpose

            def transpose_x(k):
                pe.wait_ge(d_x[k], 16)
                if k >= 3:
                    pe.wait_ge(s_res, k - 2)
                for i, t in enumerate(tiles(k)):
                    ins = tr(XT[:, i * P:(i + 1) * P], x_all[:, t, :], ident[:, :])
                ins.then_inc(p_xT, 1)

            def spread(c):
                pe.wait_ge(s_diag, c + 1)
                if c:
                    pe.wait_ge(s_v, c)
                mm(OT[:, :], ones[:, :], diag, start=True, stop=True).then_inc(p_rs, 1)

            def transpose_y(k):
                pe.wait_ge(s_yr, k + 1)
                if k >= 3:
                    pe.wait_ge(s_key, k - 2)
                b = batch_of(k - 3) if k >= 3 else 0
                if k >= 3 and k - 3 == FIRST[b + 1] - 1:
                    pe.wait_ge(s_woff, b + 1)
                for i in range(CT):
                    ins = tr(HT[:, i * P:(i + 1) * P], yr[:, i * P:(i + 1) * P], ident[:, :])
                if k % SC < SC - 1:
                    pe.wait_ge(s_ycol, k // SC + 1)
                    ins = mm(MI[:, M_YB:M_YB + 1], x_all[:, (k + 1) * CT, :], ycol[:, :], start=True, stop=True)
                ins.then_inc(p_yT, 1)

            def square_sums(k):
                pe.wait_ge(s_sq2, k + 1)
                for i in range(CT):
                    ins = mm(MI[:, M_SS + i:M_SS + i + 1], x2q[:, i * P:(i + 1) * P], ones[:, 0:1], start=True,
                             stop=True)
                ins.then_inc(p_ss2, 1)

            def mlp_block(c, m):
                pe.wait_ge(s_z, c + 1)
                if m >= 2:
                    pe.wait_ge(s_h, NM * c + m - 1)
                elif c >= 2:
                    pe.wait_ge(s_sh, SJ * (c - 2) + m + 1)
                mm(GU[:, 2 * (m % 2), :], wgate_sb[:, m * P:(m + 1) * P], zT, start=True, stop=True)
                mm(GU[:, 2 * (m % 2) + 1, :], wup_sb[:, m * P:(m + 1) * P], zT, start=True, stop=True).then_inc(p_gu, 1)

            def mlp_base(c):
                mm(OT[:, :], ones[0:1, :], bdown_sb[:, :].unsqueeze(1).to_broadcast([1, CT, P]),
                   start=True, stop=False, skip_group_check=True)
                for i in range(CT):
                    tok = slice(i * P, (i + 1) * P)
                    mm(OT[:, tok], x2T[:, c % 2, tok], ident[:, :], start=False, stop=False, skip_group_check=True)

            def mlp_down(c, m):
                pe.wait_ge(s_h, NM * c + m + 1)
                for i in range(CT):
                    tok = slice(i * P, (i + 1) * P)
                    ins = mm(OT[:, tok], h_sb[:, m, tok], wdown_sb[:, m, :], start=False, stop=(m == NM - 1),
                             skip_group_check=True)
                if m == NM - 1:
                    ins.then_inc(p_dn, 1)

            def transpose_x1(c, k):
                pe.wait_ge(s_x1r, c + 1)
                if k < NC:
                    pe.wait_ge(s_xT, k + 1)
                elif c:
                    pe.wait_ge(s_res, c)
                for i, t in enumerate(tiles(c)):
                    ins = tr(XT[:, i * P:(i + 1) * P], x1r[:, t, :], ident[:, :])
                ins.then_inc(p_x1, 1)

            def logits(c):
                pe.wait_ge(s_x1T, c + 1)
                for i in range(CT):
                    ins = mm(MI[:, M_LG + i * E:M_LG + (i + 1) * E], x1T[:, i * P:(i + 1) * P], gatew_sb[:, :],
                             start=True, stop=True)
                ins.then_inc(p_lg, 1)

            def ranks(c, k):
                b = batch_of(c)
                pe.wait_ge(s_sel, c + 1)
                if k < NC:
                    pe.wait_ge(s_yT, k + 1)
                else:
                    pe.wait_ge(s_key, c)
                for f in range(FIRST[b], c):
                    for t in range(f % 4 * CT, (f % 4 + 1) * CT):
                        mm(HT[:, 0:CT * E], ones_bf[:, :], sel[:, t, :].unsqueeze(1).to_broadcast([P, CT, E]),
                           start=(f == FIRST[b] and t % CT == 0), stop=False, skip_group_check=True)
                for i in range(CT - 1):
                    n = CT - 1 - i
                    mm(HT[:, (i + 1) * E:CT * E], ones_bf[:, :],
                       sel[:, c % 4 * CT + i, :].unsqueeze(1).to_broadcast([P, n, E]),
                       start=(c == FIRST[b] and i == 0), stop=False, skip_group_check=True)
                ins = mm(HT[:, 0:CT * E], before_bf[:, :], flat(sel[:, ring(c), :]), start=False, stop=True,
                         skip_group_check=True)
                if c == FIRST[b + 1] - 1:
                    n = BATCHES[b] * CT
                    for i in range(n):
                        t = (FIRST[b] * CT + i) % (4 * CT)
                        ins = mm(HT[0:E, H_CNT:H_CNT + 1], sel[:, t, :], ones_bf[:, 0:1], start=(i == 0),
                                 stop=(i == n - 1), skip_group_check=True)
                ins.then_inc(p_rank, 1)

            def starts(b):
                pe.wait_ge(s_nt, b + 1)
                mm(HT[:, H_START:H_START + E], ntile_bf[:, :].to_broadcast([E, P]), before_bf[0:E, 0:E], start=True,
                   stop=True)
                mm(HT[0:E, H_END:H_END + 1], before_bf[0:E, 0:E], ntile_bf[:, :], start=True, stop=False)
                mm(HT[0:E, H_END:H_END + 1], ident_bf[:, :], ntile_bf[:, :], start=False,
                   stop=True).then_inc(p_start, 1)

            def tile_experts(b):
                pe.wait_ge(s_ended, b + 1)
                mm(HT[0:1, 0:ET[b]], ones_bf[0:E, 0:1], ended[:, 0:ET[b]], start=True,
                   stop=True).then_inc(p_erow, 1)

            def shared_block(c, j, k):
                if k - 1 < NC:
                    pe.wait_ge(s_h, NM * (k - 1) + 3 + j)
                else:
                    pe.wait_ge(s_sh, SJ * (c - 1) + j + 1)
                mm(GU[0:I, 2 * j, :], sgu_sb[:, 0, j, :], x1T, start=True, stop=True)
                mm(GU[0:I, 2 * j + 1, :], sgu_sb[:, 1, j, :], x1T, start=True, stop=True).then_inc(p_sh, 1)

            def shared_down(c):
                pe.wait_ge(s_sh, SJ * (c + 1))
                for i in range(CT):
                    tok = slice(i * P, (i + 1) * P)
                    for j in range(SJ):
                        ins = mm(XT[:, tok], hs[0:I, j, tok], sd_sb[:, j, :], start=(j == 0), stop=(j == SJ - 1))
                ins.then_inc(p_sd, 1)

            def step(k):
                front, mlp, route = k < NC, 0 <= k - 1 < NC, k >= 2
                if front:
                    transpose_x(k)
                if mlp:
                    spread(k - 1)
                if front:
                    transpose_y(k)
                if route:
                    transpose_x1(k - 2, k)
                if mlp:
                    if k == 1:
                        pe.wait_ge(s_mlpw, 48)
                    mlp_block(k - 1, 0)
                    mlp_block(k - 1, 1)
                if route:
                    if k == 2:
                        pe.wait_ge(s_shw, 64)
                    logits(k - 2)
                if mlp:
                    mlp_block(k - 1, 2)
                if front:
                    square_sums(k)
                if mlp:
                    mlp_base(k - 1)
                    mlp_block(k - 1, 3)
                    for m in range(NM):
                        mlp_down(k - 1, m)
                if route:
                    c = k - 2
                    shared_block(c, 0, k)
                    shared_block(c, 1, k)
                    ranks(c, k)
                    b = batch_of(c)
                    if c == FIRST[b + 1] - 1:
                        starts(b)
                        tile_experts(b)
                    shared_down(c)

            pe.wait_ge(s_const, 2)
            for k in range(NC + 2):
                step(k)

            def weight_starts(q, which, size):
                return nc.values_load_multi_w_load_instructions(
                    woff[0:1, which, bass.ds(q * QUAD, QUAD)], engines=[mybir.EngineType.PE],
                    min_val=0, max_val=(E - 1) * size,
                    skip_runtime_bounds_check_because="expert numbers are clamped to E - 1")[1]

            def is_at_least(q, n):
                return not isinstance(q, int) or q >= n

            def tr_x(q, u):
                pe.wait_ge(d_ld[u % 4], (q // 4 + 1) * 16 if isinstance(q, int) else (q - u) * 4 + 16 * (u // 4 + 1))
                if is_at_least(q, 1):
                    pe.wait_ge(s_xg, q)
                for i in range(QUAD):
                    ins = tr(XT[:, i * P:(i + 1) * P], xl[:, u % 4, i * P:(i + 1) * P], ident[:, :])
                ins.then_inc(p_tx, 1)

            def gate_up(q, u):
                at = weight_starts(q, 0, 2 * I)
                if isinstance(q, int) and q == NQ - 1:
                    pe.wait_ge(s_xg, NQ)
                for i in range(QUAD):
                    r = u % 2
                    ins = mm(GU[:, 2 * r + i // 2, (i % 2) * 2 * I:(i % 2 + 1) * 2 * I], xg[:, r, i * P:(i + 1) * P],
                             wgu_sb[:, bass.ds(at[i], 2 * I)], start=True, stop=True)
                ins.then_inc(p_eg, 1)

            def tr_h(q, u):
                pe.wait_ge(s_eh, q + 1)
                if is_at_least(q, 1):
                    pe.wait_ge(s_ht, q)
                for i in range(QUAD):
                    ins = tr(HT[0:I, i * P:(i + 1) * P], eh[:, u % 2, i * I:(i + 1) * I], ident[:, :])
                ins.then_inc(p_th, 1)

            def down(q, u):
                at = weight_starts(q, 1, P)
                if isinstance(q, int) and q == NQ - 1:
                    pe.wait_ge(s_ht, NQ)
                if is_at_least(q, 1):
                    pe.wait_ge(s_eo, q)
                for i in range(QUAD):
                    ins = mm(OT[:, i * P:(i + 1) * P], hT[0:I, u % 2, i * P:(i + 1) * P],
                             wd_sb[:, bass.ds(at[i], P)], start=True, stop=True)
                ins.then_inc(p_eo, 1)

            def quad(q, u):
                if not (isinstance(q, int) and q + 2 >= NQ):
                    tr_x(q + 2, u + 2)
                if not (isinstance(q, int) and q + 1 >= NQ):
                    gate_up(q + 1, u + 1)
                tr_h(q, u)
                if not (isinstance(q, int) and q == 0):
                    down(q - 1, u + 3)

            pe.wait_ge(s_res, NC)
            pe.wait_ge(s_woff, NBAT)
            pe.wait_ge(s_expw, 32)
            tr_x(0, 0)
            tr_x(1, 1)
            gate_up(0, 0)
            for q in range(UN):
                quad(q, q)
            with pe.Fori(1, NQ // UN - 1) as i:
                for u in range(UN):
                    quad(i * UN + u, u)
            for q in range(NQ - UN, NQ):
                quad(q, q % UN)
            down(NQ - 1, NQ - 1)

        @block.scalar
        def _(act):
            f = nc.scalar.activation

            act.wait_ge(s_par, 32)
            f(tanh_a[:, :], vec[:, V_A:V_A + 1], ACT.Tanh).then_inc(s_cact, 1)
            act.wait_ge(s_cdve, 1)
            act.wait_ge(s_const, 2)

            def row_squares(c):
                act.wait_ge(d_x[c], 16)
                if c >= NM:
                    act.wait_ge(s_ss1, c - NM + 1)
                for i, t in enumerate(tiles(c)):
                    ins = f(h_sb[:, c % NM, i * P:(i + 1) * P], x_all[:, t, :], ACT.Square, accum_out=ss1[:, t:t + 1])
                ins.then_inc(s_ss1, 1)

            def roots(k):
                lo, hi = {0: (0, 2), 1: (2, NC)}.get(k, (0, 0))
                if hi:
                    act.wait_ge(s_ss1, hi)
                    ins = f(root[:, 0, lo * CT:hi * CT], ss1[:, lo * CT:hi * CT], ACT.Sqrt, bias=eps[:, 0:1],
                            scale=1.0 / P)
                if 0 <= k - 1 < NC:
                    act.wait_ge(p_ss2, k)
                    ins = f(root[:, 1, span(k - 1)], MI[:, M_SS:M_SS + CT], ACT.Sqrt, bias=eps[:, 0:1], scale=1.0 / P)
                if k >= 2:
                    act.wait_ge(s_mv, k - 1)
                    ins = f(root[:, 2, span(k - 2)], mv[:, span(k - 2), 1], ACT.Sqrt, bias=eps[:, 1:2])
                ins.then_inc(s_root, 1)

            def scale_rows(k, front, mlp, route):
                act.wait_ge(s_inv, k + 1)
                if mlp:
                    if k >= 2:
                        act.wait_ge(p_rs, k - 1)
                    for i, t in enumerate(tiles(k - 1)):
                        ins = f(diag[:, i * P:(i + 1) * P], ident[:, :], ACT.Copy, scale=inv[:, 1, t:t + 1])
                    ins.then_inc(s_diag, 1)
                if front:
                    if k:
                        act.wait_ge(p_yT, k)
                    for i, t in enumerate(tiles(k)):
                        ins = f(yr[:, i * P:(i + 1) * P], x_all[:, t, :], ACT.Copy, scale=inv[:, 0, t:t + 1])
                    ins.then_inc(s_yr, 1)
                    if k % SC < SC - 1:
                        t = (k + 1) * CT
                        f(ycol[:, :], ident[:, 0:1], ACT.Copy, scale=inv[:, 0, t:t + 1]).then_inc(s_ycol, 1)
                if route:
                    for i, t in enumerate(tiles(k - 2)):
                        ins = f(x1r[:, t, :], vr[:, i * P:(i + 1) * P], ACT.Identity, bias=nmean[:, t:t + 1],
                                scale=inv[:, 2, t:t + 1])
                    ins.then_inc(s_x1r, 1)

            def take_front(k):
                act.wait_ge(p_xT, k + 1)
                if k >= 2:
                    act.wait_ge(p_dn, k - 1)
                f(x2T[:, k % 2, :], XT[:, :], ACT.Identity, bias=vec[:, V_CB:V_CB + 1]).then_inc(s_xT, 1)
                act.wait_ge(p_yT, k + 1)
                ins = f(yT[:, k % 2, 1:C + 1], HT[:, :], ACT.Identity, scale=vec[:, V_NORM:V_NORM + 1])
                if k % SC < SC - 1:
                    ins = f(yT[:, k % 2, C + 1:C + 2], MI[:, M_YB:M_YB + 1], ACT.Identity,
                            scale=vec[:, V_NORM:V_NORM + 1])
                ins.then_inc(s_yT, 1)

            def silu(c, m):
                n = NM * c + m
                act.wait_ge(p_gu, n + 1)
                if m >= 2:
                    act.wait_ge(s_h, n - 1)
                elif c >= 2:
                    act.wait_ge(s_sh, SJ * (c - 2) + m + 1)
                f(sil[:, m % 2, :], GU[:, 2 * (m % 2), :], ACT.Silu, bias=vec[:, V_BG + m:V_BG + m + 1]).then_inc(s_sil, 1)

            def take_x1(c):
                act.wait_ge(p_x1, c + 1)
                if c:
                    act.wait_ge(p_sh, SJ * c)
                f(x1T, XT[:, :], ACT.Copy).then_inc(s_x1T, 1)

            def squares(k):
                act.wait_ge(s_x2, k + 1)
                f(x2q, x2T[:, k % 2, :], ACT.Square).then_inc(s_sq2, 1)

            def scores(c):
                act.wait_ge(p_lg, c + 1)
                if c:
                    act.wait_ge(s_sel, c)
                f(flat(score), MI[:, M_LG:M_LG + CT * E], ACT.Sigmoid).then_inc(s_sc, 1)

            def shared_silu(c, j, k):
                n = SJ * c + j
                act.wait_ge(p_sh, n + 1)
                if k - 1 < NC:
                    act.wait_ge(s_h, NM * (k - 1) + 3 + j)
                else:
                    act.wait_ge(s_sh, SJ * (c - 1) + j + 1)
                f(sil[0:I, j, :], GU[0:I, 2 * j, :], ACT.Silu).then_inc(s_ssil, 1)

            row_squares(0)
            row_squares(1)
            for k in range(NC + 2):
                front, mlp, route = k < NC, 0 <= k - 1 < NC, k >= 2
                roots(k)
                scale_rows(k, front, mlp, route)
                if front:
                    take_front(k)
                if k == 0:
                    for c in range(2, NC):
                        row_squares(c)
                if route:
                    take_x1(k - 2)
                    scores(k - 2)
                if mlp:
                    silu(k - 1, 0)
                    silu(k - 1, 1)
                if front:
                    squares(k)
                if mlp:
                    silu(k - 1, 2)
                    silu(k - 1, 3)
                if route:
                    shared_silu(k - 2, 0, k)
                    shared_silu(k - 2, 1, k)

            def is_at_least(q, n):
                return not isinstance(q, int) or q >= n

            def take_x(q, u):
                act.wait_ge(p_tx, q + 1)
                if is_at_least(q, 2):
                    act.wait_ge(p_eg, q - 1)
                f(xg[:, u % 2, :], XT[:, :], ACT.Copy).then_inc(s_xg, 1)

            def expert_silu(q, u):
                r = u % 2
                act.wait_ge(p_eg, q + 1)
                if is_at_least(q, 2):
                    act.wait_ge(s_eh, q - 1)
                f(eg[:, r, :].rearrange("p (a t c) -> p a t c", a=2, t=2),
                  GU[:, 2 * r:2 * r + 2, 0:4 * I].rearrange("p a (t c) -> p a t c", c=2 * I)[:, :, :, 0:I],
                  ACT.Silu).then_inc(s_eg, 1)

            def take_out(q, u):
                act.wait_ge(p_eo, q + 1)
                if not isinstance(q, int):
                    act.wait_ge(d_st[u % 4], (q - u) * 4 + 16 * (u // 4))
                elif q >= 4:
                    act.wait_ge(d_st[u % 4], 16 * (q // 4))
                f(ol[:, u % 4, :], OT[:, :], ACT.Copy).then_inc(s_eo, 1)

            def quad(q, u):
                if not (isinstance(q, int) and q + 2 >= NQ):
                    take_x(q + 2, u + 2)
                if not (isinstance(q, int) and q + 1 >= NQ):
                    expert_silu(q + 1, u + 1)
                if not (isinstance(q, int) and q == 0):
                    take_out(q - 1, u - 1)

            act.wait_ge(s_res, NC)
            for b in range(NBAT):
                act.wait_ge(d_fill[b], 16 * FILL_PARTS)
            nc.scalar.preload_act_table(ACT.Silu)
            take_x(0, 0)
            take_x(1, 1)
            expert_silu(0, 0)
            for q in range(UN):
                quad(q, q)
            with act.Fori(1, NQ // UN - 1) as i:
                for u in range(UN):
                    quad(i * UN + u, u)
            for q in range(NQ - UN, NQ):
                quad(q, q)
            take_out(NQ - 1, NQ - 1)

            for c in range(NC):
                act.wait_ge(s_cmv, c + 1)
                f(csd[:, 0, span(c)], cmv[:, span(c), 1], ACT.Sqrt, bias=eps[:, 1:2]).then_inc(s_csd, 1)

        @block.vector
        def _(dve):
            v = nc.vector
            done = [0]

            def then(ins):
                done[0] += 1
                ins.then_inc(dv, 1)
                dve.wait_ge(dv, done[0])

            def bc(ap, *shape):
                return ap.to_broadcast(list(shape))

            def vc(c):
                return vec[:, c:c + 1]

            v.memset(flat(ol[:, 0:2, :]), 0.0).then_inc(s_zero, 1)
            v.memset(yT[:, 0, 0:1], 0.0)
            v.memset(yT[:, 1, C + 1:C + 2], 0.0)
            v.memset(eps[:, 0:1], RMS_EPS)
            v.memset(eps[:, 1:2], LN_EPS).then_inc(s_cdve, 1)
            dve.wait_ge(s_const, 2)
            then(v.tensor_copy(iota_f[:, :], iota_i[:, :]))

            def reciprocals(k):
                dve.wait_ge(s_root, k + 1)
                lo, hi = {0: (0, 2), 1: (2, NC)}.get(k, (0, 0))
                if hi:
                    ins = v.reciprocal(inv[:, 0, lo * CT:hi * CT], root[:, 0, lo * CT:hi * CT])
                if k >= 2:
                    then(v.reciprocal(inv[:, 2, span(k - 2)], root[:, 2, span(k - 2)]))
                    ins = v.scalar_tensor_tensor(out=nmean[:, span(k - 2)], in0=mv[:, span(k - 2), 0], scalar=-1.0,
                                                 in1=inv[:, 2, span(k - 2)], op0=ALU.mult, op1=ALU.mult)
                if 0 <= k - 1 < NC:
                    ins = v.reciprocal(inv[:, 1, span(k - 1)], root[:, 1, span(k - 1)])
                ins.then_inc(s_inv, 1)

            def norm2(c):
                dve.wait_ge(p_rs, c + 1)
                v.scalar_tensor_tensor(out=zT, in0=x2T[:, c % 2, :], scalar=vc(V_MN), in1=OT[:, :],
                                       op0=ALU.mult, op1=ALU.mult).then_inc(s_z, 1)

            def front(k):
                r = k % 2
                dve.wait_ge(s_yT, k + 1)
                if k % SC:
                    v.tensor_copy(yT[:, 1, 0:1], yT[:, 0, C:C + 1])
                    then(v.tensor_tensor_scan(scan[:, r, :], bc(tanh_a[:, 0:1], P, C), yT[:, r, 1:C + 1],
                                              scan[:, 1 - r, C - 1:C], ALU.mult, ALU.add))
                else:
                    v.tensor_tensor_scan(scan[:, r, :], bc(tanh_a[:, 0:1], P, C), yT[:, r, 1:C + 1], 0.0,
                                         ALU.mult, ALU.add)
                dve.wait_ge(s_xT, k + 1)
                for j in range(3):
                    then(v.scalar_tensor_tensor(out=x2T[:, r, :], in0=yT[:, r, j:j + C], scalar=vc(V_CW + j),
                                                in1=x2T[:, r, :], op0=ALU.mult, op1=ALU.add))
                v.scalar_tensor_tensor(out=x2T[:, r, :], in0=scan[:, r, :], scalar=vc(V_B), in1=x2T[:, r, :],
                                       op0=ALU.mult, op1=ALU.add).then_inc(s_x2, 1)

            def hidden(c, m):
                n = NM * c + m
                dve.wait_ge(s_sil, n + 1)
                v.scalar_tensor_tensor(out=h_sb[:, m, :], in0=GU[:, 2 * (m % 2) + 1, :], scalar=vc(V_BU + m),
                                       in1=sil[:, m % 2, :], op0=ALU.add, op1=ALU.mult).then_inc(s_h, 1)

            def mlp_out(c):
                dve.wait_ge(p_dn, c + 1)
                ins = v.tensor_tensor(vr, OT[:, :], flat(x_all[:, span(c), :]), ALU.add)
                ins.then_inc(s_v, 1)
                dve.wait_ge(s_v, c + 1)
                for i in range(CT):
                    ins = v.bn_stats(stats[:, i, :], vr[:, i * P:(i + 1) * P])
                then(ins)
                for i, t in enumerate(tiles(c)):
                    ins = v.bn_aggr(mv[:, t, :], stats[:, i, :])
                ins.then_inc(s_mv, 1)

            m1, m2, ties, gs = (group[:, i, :] for i in range(4))
            by_group = "p t (g e) -> p (t g) e"
            ch4, ta4, tb4 = (a.rearrange(by_group, e=EG) for a in (choice, tab_a, tab_b))

            def group_sums(c):
                n = CT * NG
                dve.wait_ge(s_sc, c + 1)
                then(v.tensor_tensor(choice, score, bc(gbias_sb[:, :].unsqueeze(1), P, CT, E), ALU.add))
                then(v.tensor_reduce(m1, ch4, AX_X, ALU.max))
                then(v.tensor_tensor(ta4, ch4, bc(m1.unsqueeze(2), P, n, EG), ALU.is_equal))
                v.tensor_reduce(ties, ta4, AX_X, ALU.add)
                then(v.scalar_tensor_tensor(out=tb4, in0=ta4, scalar=-BIG, in1=ch4, op0=ALU.mult, op1=ALU.add))
                v.tensor_reduce(m2, tb4, AX_X, ALU.max)
                then(v.tensor_scalar(ties, ties, 1.5, -BIG, ALU.is_lt, ALU.mult))
                then(v.tensor_tensor(ties, ties, m1, ALU.add))
                then(v.tensor_tensor(m2, m2, ties, ALU.max))
                then(v.tensor_tensor(gs, m1, m2, ALU.add))

            def keep_groups():
                n = CT * NG
                g3 = gs.rearrange("p (t g) -> p t g", g=NG)
                mine = bc(g3.unsqueeze(3), P, CT, NG, NG)
                other = bc(g3.unsqueeze(2), P, CT, NG, NG)
                ta5, tb5 = (a.rearrange("p t (g e) -> p t g e", e=NG) for a in (tab_a, tab_b))
                then(v.tensor_tensor(ta5, other, mine, ALU.is_equal))
                v.tensor_tensor(tb5, other, mine, ALU.is_gt)
                then(v.tensor_tensor(ta5, ta5, bc(lower_g[:, :, :].unsqueeze(1), P, CT, NG, NG), ALU.mult))
                then(v.tensor_tensor(ta4, ta4, tb4, ALU.add))
                then(v.tensor_reduce(m1, ta4, AX_X, ALU.add))
                then(v.tensor_scalar(m2, m1, TOPG - 0.5, None, ALU.is_lt))
                then(v.tensor_tensor(ch4, ch4, bc(m2.unsqueeze(2), P, n, EG), ALU.mult))
                then(v.tensor_scalar(choice, choice, 0.0, None, ALU.add))

            def choose(c):
                for i in range(CT):
                    ins = v.max(top[:, i, :], choice[:, i, :])
                then(ins)
                for i in range(CT):
                    ins = v.match_replace(out=tab_a[:, i, :], in_to_replace=top[:, i, :], in_values=choice[:, i, :],
                                          imm_value=GONE)
                then(ins)
                if c >= 4:
                    dve.wait_ge(p_rank, c)
                then(v.tensor_scalar(sel[:, ring(c), :], tab_a, GONE, None, ALU.is_equal))
                v.tensor_tensor(tab_b, sel[:, ring(c), :], score, ALU.mult).then_inc(s_sel, 1)

            def weigh(c):
                dve.wait_ge(s_sel, c + 1)
                then(v.tensor_reduce(wsum[:, 0, :], tab_b, AX_X, ALU.add))
                then(v.tensor_scalar(wsum[:, 0, :], wsum[:, 0, :], 1e-20, None, ALU.add))
                then(v.reciprocal(wsum[:, 1, :], wsum[:, 0, :]))
                then(v.tensor_scalar(wsum[:, 1, :], wsum[:, 1, :], ROUTED_SCALE, None, ALU.mult))
                v.tensor_tensor(rw[:, span(c), :], tab_b, bc(wsum[:, 1, :].unsqueeze(2), P, CT, E), ALU.mult)
                dve.wait_ge(p_rank, c + 1)
                v.scalar_tensor_tensor(out=flat(key[:, span(c), :]), in0=HT[:, 0:CT * E], scalar=1.0,
                                       in1=flat(sel[:, ring(c), :]), op0=ALU.add, op1=ALU.mult).then_inc(s_key, 1)

            def assign_slots(b):
                then(v.tensor_scalar(ntile_i[:, 0:1], HT[0:E, H_CNT:H_CNT + 1], float(P - 1), None, ALU.add))
                then(v.tensor_scalar(ntile_i[:, 1:2], ntile_i[:, 0:1], P.bit_length() - 1, None,
                                     ALU.logical_shift_right))
                v.tensor_copy(ntile_bf[:, :], ntile_i[:, 1:2]).then_inc(s_nt, 1)
                dve.wait_ge(p_start, b + 1)
                v.tensor_copy(tile_end[:, :], HT[0:E, H_END:H_END + 1])
                then(v.tensor_scalar(start[:, :], HT[:, H_START:H_START + E], float(P), None, ALU.mult))
                for c in range(FIRST[b], FIRST[b + 1]):
                    then(v.tensor_tensor(tab_a, sel[:, ring(c), :], bc(start[:, :].unsqueeze(1), P, CT, E), ALU.mult))
                    then(v.tensor_tensor(key[:, span(c), :], key[:, span(c), :], tab_a, ALU.add))
                    for t in tiles(c):
                        ins = v.max(keys[:, t, :], key[:, t, :])
                then(ins)
                lo, hi = FIRST[b] * CT, FIRST[b + 1] * CT
                v.tensor_scalar(slots[:, lo * K:hi * K], flat(keys[:, lo:hi, :]), -1.0, None,
                                ALU.add).then_inc(s_slot, 1)
                v.tensor_scalar(ended[:, 0:ET[b]], iota_f[:, 0:ET[b]], tile_end[:, 0:1], None,
                                ALU.is_ge).then_inc(s_ended, 1)
                dve.wait_ge(p_erow, b + 1)
                row = HT[0:1, 0:ET[b]]
                v.tensor_scalar(woff[0:1, 0, ET0[b]:ET0[b + 1]], row, float(E - 1), float(2 * I), ALU.min, ALU.mult)
                v.tensor_scalar(woff[0:1, 1, ET0[b]:ET0[b + 1]], row, float(E - 1), float(P), ALU.min,
                                ALU.mult).then_inc(s_woff, 1)

            def shared_hidden(c, j):
                dve.wait_ge(s_ssil, SJ * c + j + 1)
                if c:
                    dve.wait_ge(p_sd, c)
                v.tensor_tensor(hs[0:I, j, :], GU[0:I, 2 * j + 1, :], sil[0:I, j, :], ALU.mult).then_inc(s_sh, 1)

            def shared_out(c):
                dve.wait_ge(p_sd, c + 1)
                v.tensor_tensor(flat(x_all[:, span(c), :]), XT[:, :], flat(x1r[:, span(c), :]),
                                ALU.add).then_inc(s_res, 1)

            for k in range(NC + 2):
                mlp, route = 0 <= k - 1 < NC, k >= 2
                c = k - 2
                reciprocals(k)
                if mlp:
                    norm2(k - 1)
                if k == 0:
                    dve.wait_ge(s_cact, 1)
                if k < NC:
                    front(k)
                if route:
                    group_sums(c)
                if mlp:
                    hidden(k - 1, 0)
                    hidden(k - 1, 1)
                if route:
                    keep_groups()
                if mlp:
                    hidden(k - 1, 2)
                    hidden(k - 1, 3)
                if route:
                    choose(c)
                if mlp:
                    mlp_out(k - 1)
                if route:
                    weigh(c)
                    shared_hidden(c, 0)
                    shared_hidden(c, 1)
                    if c == FIRST[batch_of(c) + 1] - 1:
                        assign_slots(batch_of(c))
                    shared_out(c)

            def is_at_least(q, n):
                return not isinstance(q, int) or q >= n

            def mul_h(q, u):
                r = u % 2
                dve.wait_ge(s_eg, q + 1)
                if is_at_least(q, 2):
                    dve.wait_ge(p_th, q - 1)
                v.tensor_tensor(
                    eh[:, r, :].rearrange("p (a t c) -> p a t c", a=2, t=2),
                    GU[:, 2 * r:2 * r + 2, 0:4 * I].rearrange("p a (t c) -> p a t c", c=2 * I)[:, :, :, I:2 * I],
                    eg[:, r, :].rearrange("p (a t c) -> p a t c", a=2, t=2), ALU.mult).then_inc(s_eh, 1)

            def take_h(q, u):
                dve.wait_ge(p_th, q + 1)
                if is_at_least(q, 2):
                    dve.wait_ge(p_eo, q - 1)
                v.tensor_copy(hT[0:I, u % 2, :], HT[0:I, :]).then_inc(s_ht, 1)

            def quad(q, u):
                if not (isinstance(q, int) and q + 1 >= NQ):
                    mul_h(q + 1, u + 1)
                take_h(q, u)

            wt3 = wtab[:, :].rearrange("p (k e) -> p k e", e=E)

            def slot_weights(t, n):
                one = bass.ds(t, 1)
                v.tensor_tensor(wt3, bc(key[:, one, :], P, K, E),
                                bc(keys[:, one, :].rearrange("p a k -> p k a"), P, K, E),
                                ALU.is_equal).then_inc(s_wk, 1)
                dve.wait_ge(s_wk, n + 1)
                v.tensor_tensor(wt3, wt3, bc(rw[:, one, :], P, K, E), ALU.mult).then_inc(s_wk, 1)
                dve.wait_ge(s_wk, n + 2)
                v.tensor_reduce(wk[:, bass.ds(t * K, K)], wt3, AX_X, ALU.add).then_inc(s_wk, 1)
                dve.wait_ge(s_wk, n + 3)

            def add_rows(c):
                def add(t, k):
                    i = t - c * CT
                    v.scalar_tensor_tensor(
                        out=x_all[:, t, :], in0=gbuf[:, c % 2, i, bass.ds(k, 1), :].rearrange("p a d -> p (a d)"),
                        scalar=wk[:, bass.ds(k + t * K, 1)], in1=x_all[:, t, :],
                        op0=ALU.mult, op1=ALU.add).then_inc(s_acc, 1)

                dve.wait_ge(d_gat[c], 16 * CT * K)
                for t in tiles(c):
                    add(t, 0)
                with dve.Fori(1, K) as k:
                    dve.wait_ge(s_acc, k * CT + CT * K * c)
                    for t in tiles(c):
                        add(t, k)

            def last_norm(c):
                dve.wait_ge(s_acc, CT * K * (c + 1))
                for i, t in enumerate(tiles(c)):
                    ins = v.bn_stats(cst[:, i, :], x_all[:, t, :])
                then(ins)
                for i, t in enumerate(tiles(c)):
                    ins = v.bn_aggr(cmv[:, t, :], cst[:, i, :])
                ins.then_inc(s_cmv, 1)
                dve.wait_ge(s_csd, c + 1)
                then(v.reciprocal(csd[:, 1, span(c)], csd[:, 0, span(c)]))
                for t in tiles(c):
                    ins = v.tensor_scalar(x_all[:, t, :], x_all[:, t, :], cmv[:, t, 0:1], csd[:, 1, t:t + 1],
                                          ALU.subtract, ALU.mult)
                ins.then_inc(s_out, 1)

            mul_h(0, 0)
            for q in range(UN):
                quad(q, q)
            for t in range(WT):
                slot_weights(t, 3 * t)
            with dve.Fori(1, SUM_AT[0]) as i:
                for u in range(UN):
                    quad(i * UN + u, u)
                    if u % 2:
                        t = u // 2
                        slot_weights(i * WT + t, i * (3 * WT) + 3 * t)
            for c, turn in enumerate(SUM_AT):
                add_rows(c)
                with dve.Fori(turn, SUM_AT[c + 1] if c + 1 < len(SUM_AT) else NQ // UN - 1) as i:
                    for u in range(UN):
                        quad(i * UN + u, u)
            for q in range(NQ - UN, NQ):
                quad(q, q)
            for c in range(len(SUM_AT)):
                last_norm(c)
            for c in range(len(SUM_AT), NC):
                add_rows(c)
                last_norm(c)


def kernel(**inputs):
    import numpy as np
    import concourse.bacc as bacc
    from concourse.bass_utils import run_bass_kernel_spmd as run

    g = {k[3:]: np.asarray(a) for k, a in inputs.items()}
    a = lambda n: g["attn_" + n]
    f = lambda n: g["ffn_" + n]
    cols = [a("norm_w"), *a("conv_w")[:, 0, :].T, a("conv_b"), a("a"), a("b"), a("mlp_norm_w"),
            *a("b_gate").reshape(NM, P), *a("b_up").reshape(NM, P)]
    ins = {
        "x": a("x"),
        "vecs": np.stack(cols, axis=1),
        "w_gate": a("w_gate"),
        "w_up": a("w_up"),
        "w_down": a("w_down"),
        "b_down": a("b_down").reshape(1, P),
        "gate_wT": f("gate_w").T,
        "gate_bias": f("gate_bias"),
        "wgu": np.concatenate([f("Wg"), f("Wu")], axis=1).transpose(2, 0, 1).reshape(P, E * 2 * I),
        "wd": f("Wd").transpose(2, 0, 1).reshape(I, E * P),
        "sgu": np.stack([f("Sg"), f("Su")]).reshape(2, SJ, I, P).transpose(3, 0, 1, 2),
        "sd": f("Sd").T.reshape(SJ, I, P).transpose(1, 0, 2),
    }
    ins = {n: np.ascontiguousarray(v) for n, v in ins.items()}
    nc = bacc.Bacc("TRN2", target_bir_lowering=False, num_devices=1)
    aps = {n: nc.dram_tensor(n + "_dram", v.shape, mybir.dt.from_np(v.dtype), kind="ExternalInput").ap()
           for n, v in ins.items()}
    out = nc.dram_tensor("out_dram", (NB, T, P), F32, kind="ExternalOutput").ap()
    xs = [nc.dram_tensor(f"xs{b}_dram", (ET[b] * P, P), F32, kind="Internal").ap() for b in range(NBAT)]
    os = [nc.dram_tensor(f"os{b}_dram", (ET[b] * P, P), F32, kind="Internal").ap() for b in range(NBAT)]
    build(nc, out=out, xs=xs, os=os, **aps)
    r = run(nc, [{n + "_dram": v for n, v in ins.items()}], core_ids=[0])
    return r.results[0]["out_dram"]
```

```python
from contextlib import ExitStack

import concourse.bass as bass
from concourse import mybir

F32 = mybir.dt.float32
BF16 = mybir.dt.bfloat16
I32 = mybir.dt.int32
U32 = mybir.dt.uint32
ALU = mybir.AluOpType
ACT = mybir.ActivationFunctionType
AX_X = mybir.AxisListType.X

P = 128
NB = 4
T = 1024
NT = NB * T // P
C = 512
CT = C // P
NC = NB * T // C
SC = T // C
HID = 512
NM = HID // P
E = 64
I = 88
K = 8
NG = 8
EG = E // NG
TOPG = 4
SJ = 2
ROUTED_SCALE = 2.5
RMS_EPS = 1e-6
LN_EPS = 1e-5
BIG = 1e30
GONE = -3e38
FAR = float(1 << 20)

BATCHES = (3, 3, 2)
NBAT = len(BATCHES)
FIRST = [sum(BATCHES[:b]) for b in range(NBAT + 1)]
LAST = [f - 1 for f in FIRST[1:]]
EARLY = LAST[0]
ET = [n * CT * K + E for n in BATCHES]
ET0 = [sum(ET[:b]) for b in range(NBAT + 1)]
QUAD = 4
NQ = ET0[-1] // QUAD
Q0 = [e // QUAD for e in ET0]
UN = 4
SUM_AT = (17, 20, 23, 25)
SUMMED = len(SUM_AT) + 2
HALF = K // 2
ROUNDS = {0: (SUMMED - 2, 0), 1: (SUMMED - 2, HALF), 3: (SUMMED - 1, 0), 4: (SUMMED - 1, HALF)}
STATS = {2: (0, 1), 5: (2, 3), 6: (4, 5)}
WT = 2
assert SUMMED == NC - 2 and WT * UN // 2 == UN and SUM_AT[0] >= NT // WT

FILL_PARTS = 4

V_NORM, V_CW, V_CB, V_A, V_B, V_MN, V_BG, V_BU = 0, 1, 4, 5, 6, 7, 8, 8 + NM
NV = 8 + 2 * NM

M_LG, M_SS, M_YB = 0, 256, 264
H_RANK, H_CNT, H_END, H_START = 0, 256, 257, 320

OUT = [(c * CT, (c + 1) * CT) for c in range(NC - 1)] + [(t, t + 1) for t in range((NC - 1) * CT, NT)]
ROOTS = [(0, SUMMED * CT)] + OUT[SUMMED:]
GROUPS = ((0, 1), (1, 2), (2, 4), (4, NC))


def group_of(c):
    return max(g for g, (lo, hi) in enumerate(GROUPS) if lo <= c)


def batch_of(c):
    return max(b for b in range(NBAT) if FIRST[b] <= c)


def build(nc, x, vecs, w_gate, w_up, w_down, b_down, gate_wT, gate_bias, wgu, wd, sgu, sd, out, xs, os):
    with ExitStack() as ctx:
        def sb(name, shape, dt=F32):
            return ctx.enter_context(nc.sbuf_tensor(name, shape, dt))

        def psum(name, shape, dt=F32):
            return ctx.enter_context(nc.psum_tensor(name, shape, dt))

        def sem(name):
            return ctx.enter_context(nc.semaphore(name))

        wgu_sb = sb("wgu_sb", [P, E * 2 * I])
        wd_sb = sb("wd_sb", [I, E * P])
        mlpw_sb = sb("mlpw_sb", [P, 3 * HID])
        wgate_sb, wup_sb = mlpw_sb[:, 0:HID], mlpw_sb[:, HID:2 * HID]
        wdown_sb = mlpw_sb[:, 2 * HID:].rearrange("p (m d) -> p m d", d=P)
        bdown_sb = sb("bdown_sb", [P, P])
        gatew_sb = sb("gatew_sb", [P, E])
        gbias_sb = sb("gbias_sb", [P, E])
        sgu_sb = sb("sgu_sb", [P, 2, SJ, I])
        sd_sb = sb("sd_sb", [I, SJ, P])
        vec = sb("vec", [P, NV])
        tanh_a = sb("tanh_a", [P, 1])
        eps = sb("eps", [P, 2])
        ident = sb("ident", [P, P])
        ones = sb("ones", [P, P])
        ident_bf = sb("ident_bf", [E, E], BF16)
        ones_bf = sb("ones_bf", [P, P], BF16)
        before_bf = sb("before_bf", [P, P], BF16)
        lower_g = sb("lower_g", [P, NG, NG])
        iota_i = sb("iota_i", [E, max(ET)], I32)
        iota_f = sb("iota_f", [E, max(ET)])

        x_all = sb("x_all", [P, NT, P])
        x1r = sb("x1r", [P, NT, P])
        slots = sb("slots", [P, NT * K], U32)
        keys = sb("keys", [P, NT, K])
        wk = sb("wk", [P, NT * K])
        rw = sb("rw", [P, NT, E])
        key = sb("key", [P, NT, E])
        woff = sb("woff", [1, 2, ET0[-1]], I32)

        sel = sb("sel", [P, 4 * CT, E], BF16)
        ss1 = sb("ss1", [P, NT])
        root = sb("root", [P, 3, NT])
        inv = sb("inv", [P, 3, NT])
        nmean = sb("nmean", [P, NT])
        ycol = sb("ycol", [P, 1])
        stats = sb("stats", [P, CT, 6])
        mv = sb("mv", [P, NT, 2])
        group = sb("group", [P, 4, CT * NG])
        top = sb("top", [P, CT, K])
        wsum = sb("wsum", [P, 2, NT])
        ntile_i = sb("ntile_i", [E, 2], I32)
        ntile_bf = sb("ntile_bf", [E, 1], BF16)
        tile_end = sb("tile_end", [E, 1])
        start = sb("start", [P, E])
        ended = sb("ended", [E, max(ET)], BF16)

        arena = sb("arena", [P, 12288])
        used = [0]

        def cut(*shape):
            size = 1
            for s in shape:
                size *= s
            lo = used[0]
            used[0] += size
            assert used[0] <= 12288
            ap = arena[:, lo:lo + size]
            if len(shape) == 2:
                return ap.rearrange("p (a b) -> p a b", b=shape[1])
            if len(shape) == 4:
                return ap.rearrange("p (a b c d) -> p a b c d", b=shape[1], c=shape[2], d=shape[3])
            return ap

        score = cut(CT, E)
        choice = cut(CT, E)
        tab_a = cut(CT, E)
        tab_b = cut(CT, E)
        yr = cut(C)
        yT = cut(2, C + 2)
        scan = cut(2, C)
        x2T = cut(2, C)
        x2q = cut(C)
        diag = cut(C)
        zT = cut(C)
        sil = cut(2, C)
        h_sb = cut(NM, C)
        vr = cut(C)
        xq = cut(C)
        x1T = cut(C)
        used[0] = 0
        gbuf = cut(2, CT, K, P)
        xl = cut(4, QUAD * P)
        xg = cut(2, QUAD * P)
        hT = cut(2, QUAD * P)
        used[0] = 2 * CT * K * P
        x1Ts = cut(2, C)
        ssil = cut(SJ, C)
        hs = cut(SJ, C)
        egh = mlpw_sb[:, 0:4 * QUAD * I].rearrange("p (a b) -> p a b", b=QUAD * I)
        eg, eh = egh[:, 0:2, :], egh[:, 2:4, :]
        ol = sb("ol", [P, 4, QUAD * P])
        wtab = sb("wtab", [P, K * E])
        cst = sb("cst", [P, CT, 6])
        cmv = sb("cmv", [P, NT, 2])
        csd = sb("csd", [P, 3, NT])

        GU = psum("GU", [P, 4, 512])
        XT = psum("XT", [P, 512])
        HT = psum("HT", [P, 512])
        OT = psum("OT", [P, 512])
        MI = psum("MI", [P, 512])

        s_vec = sem("s_vec")
        s_bd = sem("s_bd")
        s_mlpw = sem("s_mlpw")
        s_shw = sem("s_shw")
        s_expw = sem("s_expw")
        d_x = [sem(f"d_x{c}") for c in range(NC)]
        s_zero = sem("s_zero")
        d_fill = [sem(f"d_fill{b}") for b in range(NBAT)]
        s_const = sem("s_const")
        s_cdve = sem("s_cdve")
        s_cact = sem("s_cact")
        dv = sem("dv")
        s_ss1 = sem("s_ss1")
        s_root1 = sem("s_root1")
        s_inv1 = sem("s_inv1")
        s_root2 = sem("s_root2")
        s_root3 = sem("s_root3")
        s_inv3 = sem("s_inv3")
        s_ycol = sem("s_ycol")
        s_yr = sem("s_yr")
        p_xT = sem("p_xT")
        p_yT = sem("p_yT")
        s_xb = sem("s_xb")
        s_xT = sem("s_xT")
        p_yb = sem("p_yb")
        s_yb = sem("s_yb")
        s_yT = sem("s_yT")
        s_x2 = sem("s_x2")
        s_sq2 = sem("s_sq2")
        p_ss2 = sem("p_ss2")
        s_diag = sem("s_diag")
        p_rs = sem("p_rs")
        s_z = sem("s_z")
        p_gu = sem("p_gu")
        s_sil = sem("s_sil")
        s_h = sem("s_h")
        p_dn = sem("p_dn")
        s_v = sem("s_v")
        s_mv = sem("s_mv")
        s_x1r = sem("s_x1r")
        p_x1 = sem("p_x1")
        s_x1T = sem("s_x1T")
        p_lg = sem("p_lg")
        s_sc = sem("s_sc")
        s_sel = sem("s_sel")
        p_rank = sem("p_rank")
        s_key = sem("s_key")
        s_nt = sem("s_nt")
        p_start = sem("p_start")
        s_slot = sem("s_slot")
        s_ended = sem("s_ended")
        p_erow = sem("p_erow")
        s_woff = sem("s_woff")
        p_x1s = sem("p_x1s")
        s_x1s = sem("s_x1s")
        p_sh = sem("p_sh")
        s_ssil = sem("s_ssil")
        s_sh = sem("s_sh")
        p_sd = sem("p_sd")
        s_res = sem("s_res")
        s_wk = sem("s_wk")
        d_scat = [sem(f"d_scat{b}") for b in range(NBAT)]
        d_ld = [sem(f"d_ld{r}") for r in range(4)]
        d_st = [sem(f"d_st{r}") for r in range(4)]
        d_gat = [sem(f"d_gat{c}") for c in range(NC - 1)]
        d_gat_half = [sem(f"d_gat_half{i}") for i in range(2 * CT)]
        p_tx = sem("p_tx")
        s_xg = sem("s_xg")
        p_eg = sem("p_eg")
        s_eg = sem("s_eg")
        s_eh = sem("s_eh")
        p_th = sem("p_th")
        s_ht = sem("s_ht")
        p_eo = sem("p_eo")
        s_eo = sem("s_eo")
        s_acc = sem("s_acc")
        s_cmv = sem("s_cmv")
        s_csd = sem("s_csd")
        s_ncmean = sem("s_ncmean")
        s_out_a = sem("s_out_a")
        s_out = sem("s_out")
        d_out = sem("d_out")

        xs_t = [a.rearrange("(n p) d -> p n d", p=P) for a in xs]
        os_t = [a.rearrange("(n p) d -> p n d", p=P) for a in os]
        x_t = x.rearrange("b (t p) d -> p (b t) d", p=P)
        out_t = out.rearrange("b (t p) d -> p (b t) d", p=P)

        def tiles(c):
            return range(c * CT, (c + 1) * CT)

        def span(c):
            return slice(c * CT, (c + 1) * CT)

        def ring(c):
            return slice(c % 4 * CT, (c % 4 + 1) * CT)

        def flat(ap):
            return ap.rearrange("p a b -> p (a b)")

        block = ctx.enter_context(nc.Block())

        @block.sync
        def _(sp):
            def load_x(c):
                sp.dma_start(x_all[:, span(c), :], x_t[:, span(c), :]).then_inc(d_x[c], 16)

            def fill(b, parts):
                n = ET[b] * P // parts
                for i in range(parts):
                    sp.dma_start(xs[b][i * n:(i + 1) * n, :].rearrange("(p n c) d -> p n (c d)", p=P, c=K),
                                 flat(ol[:, 0:2, :]).unsqueeze(1).to_broadcast([P, n // P // K, K * P])
                                 ).then_inc(d_fill[b], 16)

            sp.dma_start(vec[:, :], vecs).then_inc(s_vec, 16)
            load_x(0)
            load_x(1)
            sp.dma_start(bdown_sb[:, :], b_down.partition_broadcast(P)).then_inc(s_bd, 16)
            sp.dma_start(wgate_sb, w_gate).then_inc(s_mlpw, 16)
            sp.dma_start(wup_sb, w_up).then_inc(s_mlpw, 16)
            sp.dma_start(wdown_sb, w_down.rearrange("(m p) d -> p m d", p=P)).then_inc(s_mlpw, 16)
            for c in range(2, NC):
                load_x(c)
            sp.dma_start(gatew_sb[:, :], gate_wT).then_inc(s_shw, 16)
            sp.dma_start(gbias_sb[:, :], gate_bias.partition_broadcast(P)).then_inc(s_shw, 16)
            sp.dma_start(sgu_sb[:, :, :, :], sgu).then_inc(s_shw, 16)
            sp.dma_start(sd_sb[:, :, :], sd).then_inc(s_shw, 16)
            sp.wait_ge(s_zero, 1)
            fill(0, FILL_PARTS)
            sp.dma_start(wgu_sb[:, :], wgu).then_inc(s_expw, 16)
            sp.dma_start(wd_sb[:, :], wd).then_inc(s_expw, 16)
            for b in range(1, NBAT):
                fill(b, FILL_PARTS)

            def load(b, q, u):
                sp.dma_start(xl[:, u % 4, :].rearrange("p (t d) -> p t d", d=P),
                             xs_t[b][:, bass.ds(q * QUAD, QUAD), :]).then_inc(d_ld[u % 4], 16)

            def store(b, q, u):
                sp.wait_ge(s_eo, q + (Q0[b] + 1))
                sp.dma_start(os_t[b][:, bass.ds(q * QUAD, QUAD), :],
                             ol[:, u % 4, :].rearrange("p (t d) -> p t d", d=P)).then_inc(d_st[u % 4], 16)

            def load_next(q):
                if q + 4 < NQ:
                    b = max(i for i in range(NBAT) if Q0[i] <= q + 4)
                    if q + 4 == Q0[b]:
                        sp.wait_ge(d_scat[b], 16 * BATCHES[b] * CT * K)
                    sp.wait_ge(p_tx, q + 1)
                    load(b, q + 4 - Q0[b], q)

            def store_last(q):
                if q >= 3:
                    b = max(i for i in range(NBAT) if Q0[i] <= q - 3)
                    store(b, q - 3 - Q0[b], q + 1)

            sp.wait_ge(s_x1r, NC)
            sp.wait_ge(d_scat[0], 16 * BATCHES[0] * CT * K)
            for q in range(4):
                load(0, q, q)
            for b in range(NBAT):
                for q in range(Q0[b], Q0[b] + 4):
                    load_next(q)
                    store_last(q)
                with sp.Fori(1, (Q0[b + 1] - Q0[b]) // 4 - 1) as i:
                    for u in range(4):
                        sp.wait_ge(p_tx, i * 4 + (Q0[b] + u + 1))
                        load(b, i * 4 + (u + 4), u)
                        store(b, i * 4 + (u - 3), u + 1)
                for q in range(Q0[b + 1] - 4, Q0[b + 1]):
                    load_next(q)
                    store_last(q)
            for q in range(NQ, NQ + 3):
                store_last(q)

            for n, (lo, hi) in enumerate(OUT):
                if n < SUMMED:
                    sp.wait_ge(s_out_a, n + 1)
                else:
                    sp.wait_ge(s_out, n - SUMMED + 1)
                sp.dma_start(out_t[:, lo:hi, :], x_all[:, lo:hi, :]).then_inc(d_out, 16)
            sp.wait_ge(d_out, 16 * len(OUT))

        @block.gpsimd
        def _(pool):
            g = nc.gpsimd
            g.memset(ident[:, :], 0.0)
            g.memset(ones[:, :], 1.0)
            g.memset(ident_bf[:, :], 0.0)
            g.memset(ones_bf[:, :], 1.0)
            g.memset(before_bf[:, :], 1.0)
            g.memset(lower_g[:, :, :], 1.0).then_inc(s_const, 1)
            pool.wait_ge(s_const, 1)
            g.affine_select(out=ident[:, :], in_=ident[:, :], compare_op=ALU.not_equal, fill=1.0, base=0,
                            pattern=[[-1, P]], channel_multiplier=1)
            g.affine_select(out=ident_bf[:, :], in_=ident_bf[:, :], compare_op=ALU.not_equal, fill=1.0, base=0,
                            pattern=[[-1, E]], channel_multiplier=1)
            g.affine_select(out=before_bf[:, :], in_=before_bf[:, :], compare_op=ALU.is_gt, fill=0.0, base=0,
                            pattern=[[1, P]], channel_multiplier=-1)
            g.affine_select(out=lower_g[:, :, :], in_=lower_g[:, :, :], compare_op=ALU.is_gt, fill=0.0, base=0,
                            pattern=[[1, NG], [-1, NG]], channel_multiplier=0)
            g.iota(iota_i[:, :], pattern=[[1, max(ET)]], base=0, channel_multiplier=0).then_inc(s_const, 1)

            pool.wait_ge(s_bd, 16)
            for c in range(NC):
                pool.wait_ge(d_x[c], 16)
                g.tensor_tensor(x1r[:, span(c), :], x_all[:, span(c), :],
                                bdown_sb[:, :].unsqueeze(1).to_broadcast([P, CT, P]), ALU.add).then_inc(s_xb, 1)

            for b in range(NBAT):
                pool.wait_ge(s_x1r, FIRST[b + 1])
                pool.wait_ge(s_slot, b + 1)
                pool.wait_ge(d_fill[b], 16 * FILL_PARTS)
                for t in range(FIRST[b] * CT, FIRST[b + 1] * CT):
                    for k in range(K):
                        c = t * K + k
                        g.indirect_dma_start(
                            out=xs[b], out_offset=bass.IndirectOffsetOnAxis(ap=slots[:, c:c + 1], axis=0),
                            in_=x1r[:, t, :], in_offset=None).then_inc(d_scat[b], 16)

            def gather(c, i, k):
                col = (c * CT + i) * K + k
                return g.indirect_dma_start(
                    out=gbuf[:, c % 2, i, k, :], out_offset=None, in_=os[batch_of(c)],
                    in_offset=bass.IndirectOffsetOnAxis(ap=slots[:, col:col + 1], axis=0))

            for c in range(NC):
                b = batch_of(c)
                if c == FIRST[b]:
                    for r in range(4):
                        pool.wait_ge(d_st[r], 4 * Q0[b + 1])
                if c < NC - 1:
                    for k in range(K):
                        if c >= 2:
                            pool.wait_ge(s_acc, CT * K * (c - 2) + CT * (k + 1))
                        for i in range(CT):
                            gather(c, i, k).then_inc(d_gat[c], 16)
                else:
                    pool.wait_ge(s_acc, CT * K * (c - 1))
                    for i in range(CT):
                        for k in range(K):
                            gather(c, i, k).then_inc(d_gat_half[2 * i + k // HALF], 16)

        @block.tensor
        def _(pe):
            mm = nc.tensor.matmul
            tr = nc.tensor.transpose

            def transpose_x(k):
                pe.wait_ge(d_x[k], 16)
                if k >= 3:
                    pe.wait_ge(s_x1T, k - 2)
                elif k:
                    pe.wait_ge(s_xT, k)
                for i, t in enumerate(tiles(k)):
                    ins = tr(XT[:, i * P:(i + 1) * P], x_all[:, t, :], ident[:, :])
                ins.then_inc(p_xT, 1)

            def spread(c):
                pe.wait_ge(s_diag, c + 1)
                if c:
                    pe.wait_ge(s_h, NM * c - 1)
                mm(GU[:, 0, :], ones[:, :], diag, start=True, stop=True).then_inc(p_rs, 1)

            def transpose_y(k):
                pe.wait_ge(s_yr, k + 1)
                if k >= 2:
                    pe.wait_ge(s_v, k - 1)
                elif k:
                    pe.wait_ge(s_yT, k)
                for i in range(CT):
                    ins = tr(OT[:, i * P:(i + 1) * P], yr[:, i * P:(i + 1) * P], ident[:, :])
                ins.then_inc(p_yT, 1)

            def neighbour(k):
                if k < NC and k % SC < SC - 1:
                    pe.wait_ge(s_ycol, k // SC + 1)
                    if k >= 3:
                        pe.wait_ge(s_sc, k - 2)
                    mm(MI[:, M_YB:M_YB + 1], x_all[:, (k + 1) * CT, :], ycol[:, :], start=True,
                       stop=True).then_inc(p_yb, 1)

            def square_sums(k):
                pe.wait_ge(s_sq2, k + 1)
                if k >= 2:
                    pe.wait_ge(s_sc, k - 1)
                for i in range(CT):
                    ins = mm(MI[:, M_SS + i:M_SS + i + 1], x2q[:, i * P:(i + 1) * P], ones[:, 0:1], start=True,
                             stop=True)
                ins.then_inc(p_ss2, 1)

            def mlp_block(c, m):
                pe.wait_ge(s_z, c + 1)
                if m >= 2:
                    pe.wait_ge(s_h, NM * c + m - 1)
                mm(GU[:, 2 * (m % 2), :], wgate_sb[:, m * P:(m + 1) * P], zT, start=True, stop=True)
                mm(GU[:, 2 * (m % 2) + 1, :], wup_sb[:, m * P:(m + 1) * P], zT, start=True, stop=True).then_inc(p_gu, 1)

            def mlp_base(c):
                if c + 1 < NC:
                    pe.wait_ge(s_yT, c + 2)
                else:
                    pe.wait_ge(s_v, c)
                for i in range(CT):
                    tok = slice(i * P, (i + 1) * P)
                    mm(OT[:, tok], x2T[:, c % 2, tok], ident[:, :], start=(i == 0), stop=False, skip_group_check=True)

            def mlp_down(c, m):
                pe.wait_ge(s_h, NM * c + m + 1)
                for i in range(CT):
                    tok = slice(i * P, (i + 1) * P)
                    ins = mm(OT[:, tok], h_sb[:, m, tok], wdown_sb[:, m, :], start=False, stop=(m == NM - 1),
                             skip_group_check=True)
                if m == NM - 1:
                    ins.then_inc(p_dn, 1)

            def transpose_x1(c, k):
                pe.wait_ge(s_x1r, c + 1)
                if k < NC:
                    pe.wait_ge(s_xT, k + 1)
                else:
                    pe.wait_ge(s_x1T, c)
                for i, t in enumerate(tiles(c)):
                    ins = tr(XT[:, i * P:(i + 1) * P], x1r[:, t, :], ident[:, :])
                ins.then_inc(p_x1, 1)

            def logits(c):
                pe.wait_ge(s_x1T, c + 1)
                for i in range(CT):
                    ins = mm(MI[:, M_LG + i * E:M_LG + (i + 1) * E], x1T[:, i * P:(i + 1) * P], gatew_sb[:, :],
                             start=True, stop=True)
                ins.then_inc(p_lg, 1)

            def ranks(c):
                b = batch_of(c)
                pe.wait_ge(s_sel, c + 1)
                if c:
                    pe.wait_ge(s_key, c)
                if b and c == FIRST[b]:
                    pe.wait_ge(s_woff, b)
                for f in range(FIRST[b], c):
                    for t in range(f % 4 * CT, (f % 4 + 1) * CT):
                        mm(HT[:, 0:CT * E], ones_bf[:, :], sel[:, t, :].unsqueeze(1).to_broadcast([P, CT, E]),
                           start=(f == FIRST[b] and t % CT == 0), stop=False, skip_group_check=True)
                for i in range(CT - 1):
                    n = CT - 1 - i
                    mm(HT[:, (i + 1) * E:CT * E], ones_bf[:, :],
                       sel[:, c % 4 * CT + i, :].unsqueeze(1).to_broadcast([P, n, E]),
                       start=(c == FIRST[b] and i == 0), stop=False, skip_group_check=True)
                ins = mm(HT[:, 0:CT * E], before_bf[:, :], flat(sel[:, ring(c), :]), start=False, stop=True,
                         skip_group_check=True)
                if c in LAST:
                    n = BATCHES[b] * CT
                    for i in range(n):
                        t = (FIRST[b] * CT + i) % (4 * CT)
                        ins = mm(HT[0:E, H_CNT:H_CNT + 1], sel[:, t, :], ones_bf[:, 0:1], start=(i == 0),
                                 stop=(i == n - 1), skip_group_check=True)
                ins.then_inc(p_rank, 1)

            def starts(b):
                pe.wait_ge(s_nt, b + 1)
                mm(HT[:, H_START:H_START + E], ntile_bf[:, :].to_broadcast([E, P]), before_bf[0:E, 0:E], start=True,
                   stop=True)
                mm(HT[0:E, H_END:H_END + 1], before_bf[0:E, 0:E], ntile_bf[:, :], start=True, stop=False)
                mm(HT[0:E, H_END:H_END + 1], ident_bf[:, :], ntile_bf[:, :], start=False,
                   stop=True).then_inc(p_start, 1)

            def tile_experts(b):
                pe.wait_ge(s_ended, b + 1)
                mm(HT[0:1, 0:ET[b]], ones_bf[0:E, 0:1], ended[:, 0:ET[b]], start=True,
                   stop=True).then_inc(p_erow, 1)

            def step(k):
                front, mlp, route = k < NC, 1 <= k <= NC, 2 <= k < NC + 2
                c = k - 2
                if k == 0:
                    transpose_y(1)
                if k == 1:
                    pe.wait_ge(s_mlpw, 48)
                if k == 2:
                    pe.wait_ge(s_shw, 64)
                if mlp:
                    mlp_block(k - 1, 0)
                if route:
                    transpose_x1(c, k)
                if c == EARLY:
                    logits(c)
                if mlp:
                    mlp_block(k - 1, 1)
                if route and c != EARLY:
                    logits(c)
                if c >= 1 and c - 1 != EARLY:
                    ranks(c - 1)
                if mlp:
                    mlp_block(k - 1, 2)
                if c - 1 in LAST[1:]:
                    starts(batch_of(c - 1))
                if mlp:
                    mlp_block(k - 1, 3)
                    mlp_base(k - 1)
                neighbour(k + 1)
                if c == EARLY:
                    for m in range(NM // 2):
                        mlp_down(k - 1, m)
                    ranks(c)
                    starts(0)
                    for m in range(NM // 2, NM):
                        mlp_down(k - 1, m)
                if front:
                    square_sums(k)
                if mlp and c != EARLY:
                    for m in range(NM):
                        mlp_down(k - 1, m)
                if c - 1 in LAST:
                    tile_experts(batch_of(c - 1))
                if front:
                    spread(k)
                if k + 1 < NC:
                    transpose_x(k + 1)
                if k and k + 1 < NC:
                    transpose_y(k + 1)

            pe.wait_ge(s_const, 2)
            transpose_x(0)
            transpose_y(0)
            neighbour(0)
            for k in range(NC + 2):
                step(k)
            ranks(NC - 1)
            starts(NBAT - 1)

            def weight_starts(q, which, size):
                return nc.values_load_multi_w_load_instructions(
                    woff[0:1, which, bass.ds(q * QUAD, QUAD)], engines=[mybir.EngineType.PE],
                    min_val=0, max_val=(E - 1) * size,
                    skip_runtime_bounds_check_because="expert numbers are clamped to E - 1")[1]

            def is_at_least(q, n):
                return not isinstance(q, int) or q >= n

            def tr_x(q, u):
                pe.wait_ge(d_ld[u % 4], (q // 4 + 1) * 16 if isinstance(q, int) else (q - u) * 4 + 16 * (u // 4 + 1))
                if is_at_least(q, 1):
                    pe.wait_ge(s_xg, q)
                for i in range(QUAD):
                    ins = tr(XT[:, i * P:(i + 1) * P], xl[:, u % 4, i * P:(i + 1) * P], ident[:, :])
                ins.then_inc(p_tx, 1)

            def gate_up(q, u):
                at = weight_starts(q, 0, 2 * I)
                if isinstance(q, int) and q == NQ - 1:
                    pe.wait_ge(s_xg, NQ)
                for i in range(QUAD):
                    r = u % 2
                    ins = mm(GU[:, 2 * r + i // 2, (i % 2) * 2 * I:(i % 2 + 1) * 2 * I], xg[:, r, i * P:(i + 1) * P],
                             wgu_sb[:, bass.ds(at[i], 2 * I)], start=True, stop=True)
                ins.then_inc(p_eg, 1)

            def tr_h(q, u):
                pe.wait_ge(s_eh, q + 1)
                if is_at_least(q, 1):
                    pe.wait_ge(s_ht, q)
                for i in range(QUAD):
                    ins = tr(HT[0:I, i * P:(i + 1) * P], eh[:, u % 2, i * I:(i + 1) * I], ident[:, :])
                ins.then_inc(p_th, 1)

            def down(q, u):
                at = weight_starts(q, 1, P)
                if isinstance(q, int) and q == NQ - 1:
                    pe.wait_ge(s_ht, NQ)
                if is_at_least(q, 1):
                    pe.wait_ge(s_eo, q)
                for i in range(QUAD):
                    ins = mm(OT[:, i * P:(i + 1) * P], hT[0:I, u % 2, i * P:(i + 1) * P],
                             wd_sb[:, bass.ds(at[i], P)], start=True, stop=True)
                ins.then_inc(p_eo, 1)

            def quad(q, u):
                if not (isinstance(q, int) and q + 2 >= NQ):
                    tr_x(q + 2, u + 2)
                if not (isinstance(q, int) and q + 1 >= NQ):
                    gate_up(q + 1, u + 1)
                tr_h(q, u)
                if not (isinstance(q, int) and q == 0):
                    down(q - 1, u + 3)

            pe.wait_ge(s_x1T, NC)
            pe.wait_ge(s_v, NC)
            pe.wait_ge(s_woff, NBAT - 1)
            pe.wait_ge(s_expw, 32)
            tr_x(0, 0)
            tr_x(1, 1)
            gate_up(0, 0)
            tile_experts(NBAT - 1)
            pe.wait_ge(s_woff, NBAT)
            for q in range(UN):
                quad(q, q)
            with pe.Fori(1, NQ // UN - 1) as i:
                for u in range(UN):
                    quad(i * UN + u, u)
            for q in range(NQ - UN, NQ):
                quad(q, q % UN)
            down(NQ - 1, NQ - 1)

            def transpose_x1_again(c):
                if c:
                    pe.wait_ge(s_x1s, c)
                for i, t in enumerate(tiles(c)):
                    ins = tr(XT[:, i * P:(i + 1) * P], x1r[:, t, :], ident[:, :])
                ins.then_inc(p_x1s, 1)

            def shared_block(c, j):
                pe.wait_ge(s_x1s, c + 1)
                if c:
                    pe.wait_ge(s_sh, SJ * (c - 1) + j + 1)
                mm(GU[0:I, 2 * j, :], sgu_sb[:, 0, j, :], x1Ts[:, c % 2, :], start=True, stop=True)
                mm(GU[0:I, 2 * j + 1, :], sgu_sb[:, 1, j, :], x1Ts[:, c % 2, :], start=True,
                   stop=True).then_inc(p_sh, 1)

            def shared_down(c):
                pe.wait_ge(s_sh, SJ * (c + 1))
                if c == 0:
                    pe.wait_ge(s_eo, NQ)
                elif c >= 2:
                    pe.wait_ge(s_res, c - 1)
                dst = HT if c % 2 else OT
                for i in range(CT):
                    tok = slice(i * P, (i + 1) * P)
                    for j in range(SJ):
                        ins = mm(dst[:, tok], hs[0:I, j, tok], sd_sb[:, j, :], start=(j == 0), stop=(j == SJ - 1))
                ins.then_inc(p_sd, 1)

            pe.wait_ge(s_shw, 64)
            transpose_x1_again(0)
            for c in range(NC):
                if c + 1 < NC:
                    transpose_x1_again(c + 1)
                for j in range(SJ):
                    shared_block(c, j)
                if c:
                    shared_down(c - 1)
            shared_down(NC - 1)

        @block.scalar
        def _(act):
            f = nc.scalar.activation

            act.wait_ge(s_vec, 16)
            f(tanh_a[:, :], vec[:, V_A:V_A + 1], ACT.Tanh).then_inc(s_cact, 1)
            nc.scalar.preload_act_table(ACT.Sqrt)
            act.wait_ge(s_cdve, 1)
            act.wait_ge(s_const, 2)

            def row_squares(c):
                act.wait_ge(d_x[c], 16)
                if c:
                    act.wait_ge(s_ss1, c)
                for i, t in enumerate(tiles(c)):
                    ins = f(xq[:, i * P:(i + 1) * P], x_all[:, t, :], ACT.Square, accum_out=ss1[:, t:t + 1])
                ins.then_inc(s_ss1, 1)

            def root_x(g):
                lo, hi = GROUPS[g]
                act.wait_ge(s_ss1, hi)
                f(root[:, 0, lo * CT:hi * CT], ss1[:, lo * CT:hi * CT], ACT.Sqrt, bias=eps[:, 0:1],
                  scale=1.0 / P).then_inc(s_root1, 1)

            def root_x2(c):
                act.wait_ge(p_ss2, c + 1)
                f(root[:, 1, span(c)], MI[:, M_SS:M_SS + CT], ACT.Sqrt, bias=eps[:, 0:1],
                  scale=1.0 / P).then_inc(s_root2, 1)

            def root_v(c):
                act.wait_ge(s_mv, c + 1)
                f(root[:, 2, span(c)], mv[:, span(c), 1], ACT.Sqrt, bias=eps[:, 1:2]).then_inc(s_root3, 1)

            def norm_x(k):
                act.wait_ge(s_inv1, group_of(k) + 1)
                if k:
                    act.wait_ge(p_yT, k)
                for i, t in enumerate(tiles(k)):
                    ins = f(yr[:, i * P:(i + 1) * P], x_all[:, t, :], ACT.Copy, scale=inv[:, 0, t:t + 1])
                ins.then_inc(s_yr, 1)

            def neighbour(k):
                if k < NC and k % SC < SC - 1:
                    if k:
                        act.wait_ge(p_yb, k // SC)
                    t = (k + 1) * CT
                    act.wait_ge(s_inv1, group_of(k + 1) + 1)
                    f(ycol[:, :], ident[:, 0:1], ACT.Copy, scale=inv[:, 0, t:t + 1]).then_inc(s_ycol, 1)

            def norm_v(c):
                act.wait_ge(s_inv3, c + 1)
                for i, t in enumerate(tiles(c)):
                    ins = f(x1r[:, t, :], vr[:, i * P:(i + 1) * P], ACT.Identity, bias=nmean[:, t:t + 1],
                            scale=inv[:, 2, t:t + 1])
                ins.then_inc(s_x1r, 1)

            def take_y(k):
                act.wait_ge(p_yT, k + 1)
                if k >= 2:
                    act.wait_ge(s_x2, k - 1)
                f(yT[:, k % 2, 1:C + 1], OT[:, :], ACT.Identity, scale=vec[:, V_NORM:V_NORM + 1]).then_inc(s_yT, 1)

            def take_neighbour(k):
                if k % SC < SC - 1:
                    act.wait_ge(p_yb, k // SC + 1)
                    f(yT[:, k % 2, C + 1:C + 2], MI[:, M_YB:M_YB + 1], ACT.Identity,
                      scale=vec[:, V_NORM:V_NORM + 1]).then_inc(s_yb, 1)

            def take_x(k):
                act.wait_ge(p_xT, k + 1)
                if k >= 2:
                    act.wait_ge(p_dn, k - 1)
                f(x2T[:, k % 2, :], XT[:, :], ACT.Identity, bias=vec[:, V_CB:V_CB + 1]).then_inc(s_xT, 1)

            def silu(c, m):
                n = NM * c + m
                act.wait_ge(p_gu, n + 1)
                if n >= 2:
                    act.wait_ge(s_h, n - 1)
                f(sil[:, m % 2, :], GU[:, 2 * (m % 2), :], ACT.Silu, bias=vec[:, V_BG + m:V_BG + m + 1]).then_inc(s_sil, 1)

            def take_x1(c):
                act.wait_ge(p_x1, c + 1)
                if c:
                    act.wait_ge(p_lg, c)
                f(x1T, XT[:, :], ACT.Copy).then_inc(s_x1T, 1)

            def squares(k):
                act.wait_ge(s_x2, k + 1)
                f(x2q, x2T[:, k % 2, :], ACT.Square).then_inc(s_sq2, 1)

            def scores(c):
                act.wait_ge(p_lg, c + 1)
                if c:
                    act.wait_ge(s_sel, c)
                f(flat(score), MI[:, M_LG:M_LG + CT * E], ACT.Sigmoid).then_inc(s_sc, 1)

            row_squares(0)
            root_x(0)
            norm_x(0)
            row_squares(1)
            root_x(1)
            take_y(0)
            neighbour(0)
            take_x(0)
            take_neighbour(0)
            norm_x(1)
            row_squares(2)
            take_y(1)
            row_squares(3)
            for k in range(NC + 2):
                front, mlp, route = k < NC, 1 <= k <= NC, k >= 2
                if route:
                    root_v(k - 2)
                    norm_v(k - 2)
                if k - 2 == EARLY:
                    nc.scalar.preload_act_table(ACT.Sigmoid)
                    take_x1(k - 2)
                    scores(k - 2)
                if mlp:
                    nc.scalar.preload_act_table(ACT.Silu)
                if route and k - 2 != EARLY:
                    take_x1(k - 2)
                if mlp:
                    silu(k - 1, 0)
                    silu(k - 1, 1)
                neighbour(k + 1)
                if route and k - 2 != EARLY:
                    nc.scalar.preload_act_table(ACT.Sigmoid)
                    scores(k - 2)
                    nc.scalar.preload_act_table(ACT.Silu)
                if mlp:
                    silu(k - 1, 2)
                if k - 2 == EARLY:
                    silu(k - 1, 3)
                if front:
                    squares(k)
                if mlp and k - 2 != EARLY:
                    silu(k - 1, 3)
                if 1 <= k <= 2:
                    row_squares(2 * k + 2)
                    row_squares(2 * k + 3)
                nc.scalar.preload_act_table(ACT.Sqrt)
                if front:
                    root_x2(k)
                if k in (0, 2):
                    root_x(2 + k // 2)
                if k and k + 1 < NC:
                    norm_x(k + 1)
                if k + 1 < NC:
                    take_x(k + 1)
                if k and k + 1 < NC:
                    take_y(k + 1)
                if k + 1 < NC:
                    take_neighbour(k + 1)

            def is_at_least(q, n):
                return not isinstance(q, int) or q >= n

            def take_x(q, u):
                act.wait_ge(p_tx, q + 1)
                if is_at_least(q, 2):
                    act.wait_ge(p_eg, q - 1)
                f(xg[:, u % 2, :], XT[:, :], ACT.Copy).then_inc(s_xg, 1)

            def expert_silu(q, u):
                r = u % 2
                act.wait_ge(p_eg, q + 1)
                if is_at_least(q, 2):
                    act.wait_ge(s_eh, q - 1)
                f(eg[:, r, :].rearrange("p (a t c) -> p a t c", a=2, t=2),
                  GU[:, 2 * r:2 * r + 2, 0:4 * I].rearrange("p a (t c) -> p a t c", c=2 * I)[:, :, :, 0:I],
                  ACT.Silu).then_inc(s_eg, 1)

            def take_out(q, u):
                act.wait_ge(p_eo, q + 1)
                if not isinstance(q, int):
                    act.wait_ge(d_st[u % 4], (q - u) * 4 + 16 * (u // 4))
                elif q >= 4:
                    act.wait_ge(d_st[u % 4], 16 * (q // 4))
                f(ol[:, u % 4, :], OT[:, :], ACT.Copy).then_inc(s_eo, 1)

            def quad(q, u):
                if not (isinstance(q, int) and q + 2 >= NQ):
                    take_x(q + 2, u + 2)
                if not (isinstance(q, int) and q + 1 >= NQ):
                    expert_silu(q + 1, u + 1)
                if not (isinstance(q, int) and q == 0):
                    take_out(q - 1, u - 1)

            for b in range(NBAT):
                act.wait_ge(d_fill[b], 16 * FILL_PARTS)
            nc.scalar.preload_act_table(ACT.Silu)
            take_x(0, 0)
            take_x(1, 1)
            expert_silu(0, 0)
            for q in range(UN):
                quad(q, q)
            with act.Fori(1, NQ // UN - 1) as i:
                for u in range(UN):
                    quad(i * UN + u, u)
            for q in range(NQ - UN, NQ):
                quad(q, q)
            take_out(NQ - 1, NQ - 1)

            def take_x1_again(c):
                act.wait_ge(p_x1s, c + 1)
                if c >= 2:
                    act.wait_ge(p_sh, SJ * (c - 1))
                f(x1Ts[:, c % 2, :], XT[:, :], ACT.Copy).then_inc(s_x1s, 1)

            def shared_silu(c, j):
                act.wait_ge(p_sh, SJ * c + j + 1)
                if c:
                    act.wait_ge(s_sh, SJ * (c - 1) + j + 1)
                f(ssil[0:I, j, :], GU[0:I, 2 * j, :], ACT.Silu).then_inc(s_ssil, 1)

            take_x1_again(0)
            for c in range(NC):
                if c + 1 < NC:
                    take_x1_again(c + 1)
                for j in range(SJ):
                    shared_silu(c, j)

            for r, (lo, hi) in enumerate(ROOTS):
                act.wait_ge(s_cmv, SUMMED + r)
                f(csd[:, 0, lo:hi], cmv[:, lo:hi, 1], ACT.Sqrt, bias=eps[:, 1:2]).then_inc(s_csd, 1)
                if r == 0:
                    act.wait_ge(s_ncmean, 1)
                    for c in range(SUMMED):
                        for t in tiles(c):
                            ins = f(x_all[:, t, :], x_all[:, t, :], ACT.Identity, bias=csd[:, 2, t:t + 1],
                                    scale=csd[:, 1, t:t + 1])
                        ins.then_inc(s_out_a, 1)

        @block.vector
        def _(dve):
            v = nc.vector
            done = [0]

            def then(ins):
                done[0] += 1
                ins.then_inc(dv, 1)
                dve.wait_ge(dv, done[0])

            def bc(ap, *shape):
                return ap.to_broadcast(list(shape))

            def vc(c):
                return vec[:, c:c + 1]

            v.memset(flat(ol[:, 0:2, :]), 0.0).then_inc(s_zero, 1)
            v.memset(yT[:, 0, 0:1], 0.0)
            v.memset(yT[:, 1, C + 1:C + 2], 0.0)
            v.memset(eps[:, 0:1], RMS_EPS)
            v.memset(eps[:, 1:2], LN_EPS).then_inc(s_cdve, 1)
            dve.wait_ge(s_const, 2)
            then(v.tensor_copy(iota_f[:, :], iota_i[:, :]))

            def inverse_x(g):
                lo, hi = GROUPS[g]
                dve.wait_ge(s_root1, g + 1)
                v.reciprocal(inv[:, 0, lo * CT:hi * CT], root[:, 0, lo * CT:hi * CT]).then_inc(s_inv1, 1)

            def inverse_v(c):
                dve.wait_ge(s_root3, c + 1)
                then(v.reciprocal(inv[:, 2, span(c)], root[:, 2, span(c)]))
                v.scalar_tensor_tensor(out=nmean[:, span(c)], in0=mv[:, span(c), 0], scalar=-1.0,
                                       in1=inv[:, 2, span(c)], op0=ALU.mult, op1=ALU.mult).then_inc(s_inv3, 1)

            def diagonal(c):
                dve.wait_ge(s_root2, c + 1)
                then(v.reciprocal(inv[:, 1, span(c)], root[:, 1, span(c)]))
                v.tensor_tensor(diag.rearrange("p (t d) -> p t d", d=P), bc(ident[:, :].unsqueeze(1), P, CT, P),
                                bc(inv[:, 1, span(c)].unsqueeze(2), P, CT, P), ALU.mult).then_inc(s_diag, 1)

            def norm2(c):
                dve.wait_ge(p_rs, c + 1)
                v.scalar_tensor_tensor(out=zT, in0=x2T[:, c % 2, :], scalar=vc(V_MN), in1=GU[:, 0, :],
                                       op0=ALU.mult, op1=ALU.mult).then_inc(s_z, 1)

            def ssm(k):
                r = k % 2
                dve.wait_ge(s_yT, k + 1)
                if k % SC:
                    v.tensor_copy(yT[:, 1, 0:1], yT[:, 0, C:C + 1])
                    then(v.tensor_tensor_scan(scan[:, r, :], bc(tanh_a[:, 0:1], P, C), yT[:, r, 1:C + 1],
                                              scan[:, 1 - r, C - 1:C], ALU.mult, ALU.add))
                else:
                    v.tensor_tensor_scan(scan[:, r, :], bc(tanh_a[:, 0:1], P, C), yT[:, r, 1:C + 1], 0.0,
                                         ALU.mult, ALU.add)

            def conv(k):
                r = k % 2
                dve.wait_ge(s_xT, k + 1)
                if k % SC < SC - 1:
                    dve.wait_ge(s_yb, k // SC + 1)
                for j in range(3):
                    then(v.scalar_tensor_tensor(out=x2T[:, r, :], in0=yT[:, r, j:j + C], scalar=vc(V_CW + j),
                                                in1=x2T[:, r, :], op0=ALU.mult, op1=ALU.add))
                v.scalar_tensor_tensor(out=x2T[:, r, :], in0=scan[:, r, :], scalar=vc(V_B), in1=x2T[:, r, :],
                                       op0=ALU.mult, op1=ALU.add).then_inc(s_x2, 1)

            def hidden(c, m):
                n = NM * c + m
                dve.wait_ge(s_sil, n + 1)
                v.scalar_tensor_tensor(out=h_sb[:, m, :], in0=GU[:, 2 * (m % 2) + 1, :], scalar=vc(V_BU + m),
                                       in1=sil[:, m % 2, :], op0=ALU.add, op1=ALU.mult).then_inc(s_h, 1)

            def mlp_out(c):
                dve.wait_ge(p_dn, c + 1)
                dve.wait_ge(s_xb, c + 1)
                v.tensor_tensor(vr, OT[:, :], flat(x1r[:, span(c), :]), ALU.add).then_inc(s_v, 1)
                dve.wait_ge(s_v, c + 1)
                for i in range(CT):
                    ins = v.bn_stats(stats[:, i, :], vr[:, i * P:(i + 1) * P])
                then(ins)
                for i, t in enumerate(tiles(c)):
                    ins = v.bn_aggr(mv[:, t, :], stats[:, i, :])
                ins.then_inc(s_mv, 1)

            m1, m2, ties, gs = (group[:, i, :] for i in range(4))
            by_group = "p t (g e) -> p (t g) e"
            ch4, ta4, tb4 = (a.rearrange(by_group, e=EG) for a in (choice, tab_a, tab_b))

            def group_sums(c):
                n = CT * NG
                dve.wait_ge(s_sc, c + 1)
                then(v.tensor_tensor(choice, score, bc(gbias_sb[:, :].unsqueeze(1), P, CT, E), ALU.add))
                then(v.tensor_reduce(m1, ch4, AX_X, ALU.max))
                then(v.tensor_tensor(ta4, ch4, bc(m1.unsqueeze(2), P, n, EG), ALU.is_equal))
                v.tensor_reduce(ties, ta4, AX_X, ALU.add)
                then(v.scalar_tensor_tensor(out=tb4, in0=ta4, scalar=-BIG, in1=ch4, op0=ALU.mult, op1=ALU.add))

            def group_seconds():
                v.tensor_reduce(m2, tb4, AX_X, ALU.max)
                then(v.tensor_scalar(ties, ties, 1.5, -BIG, ALU.is_lt, ALU.mult))
                then(v.tensor_tensor(ties, ties, m1, ALU.add))
                then(v.tensor_tensor(m2, m2, ties, ALU.max))
                then(v.tensor_tensor(gs, m1, m2, ALU.add))

            def compare_groups():
                g3 = gs.rearrange("p (t g) -> p t g", g=NG)
                mine = bc(g3.unsqueeze(3), P, CT, NG, NG)
                other = bc(g3.unsqueeze(2), P, CT, NG, NG)
                ta5, tb5 = (a.rearrange("p t (g e) -> p t g e", e=NG) for a in (tab_a, tab_b))
                then(v.tensor_tensor(ta5, other, mine, ALU.is_equal))
                v.tensor_tensor(tb5, other, mine, ALU.is_gt)
                then(v.tensor_tensor(ta5, ta5, bc(lower_g[:, :, :].unsqueeze(1), P, CT, NG, NG), ALU.mult))

            def mask_groups():
                n = CT * NG
                then(v.tensor_tensor(ta4, ta4, tb4, ALU.add))
                then(v.tensor_reduce(m1, ta4, AX_X, ALU.add))
                then(v.tensor_scalar(m2, m1, TOPG - 0.5, None, ALU.is_lt))
                then(v.tensor_tensor(ch4, ch4, bc(m2.unsqueeze(2), P, n, EG), ALU.mult))
                then(v.tensor_scalar(choice, choice, 0.0, None, ALU.add))

            def choose(c):
                for i in range(CT):
                    ins = v.max(top[:, i, :], choice[:, i, :])
                then(ins)
                for i in range(CT):
                    ins = v.match_replace(out=tab_a[:, i, :], in_to_replace=top[:, i, :], in_values=choice[:, i, :],
                                          imm_value=GONE)
                then(ins)
                if c >= 4:
                    dve.wait_ge(p_rank, c)
                then(v.tensor_scalar(sel[:, ring(c), :], tab_a, GONE, None, ALU.is_equal))
                v.tensor_tensor(rw[:, span(c), :], sel[:, ring(c), :], score, ALU.mult).then_inc(s_sel, 1)

            def take_ranks(c):
                dve.wait_ge(p_rank, c + 1)
                v.scalar_tensor_tensor(out=flat(key[:, span(c), :]), in0=HT[:, 0:CT * E], scalar=FAR + 1.0,
                                       in1=flat(sel[:, ring(c), :]), op0=ALU.add, op1=ALU.mult).then_inc(s_key, 1)

            def count_tiles(b):
                then(v.tensor_scalar(ntile_i[:, 0:1], HT[0:E, H_CNT:H_CNT + 1], float(P - 1), None, ALU.add))
                then(v.tensor_scalar(ntile_i[:, 1:2], ntile_i[:, 0:1], P.bit_length() - 1, None,
                                     ALU.logical_shift_right))
                v.tensor_copy(ntile_bf[:, :], ntile_i[:, 1:2]).then_inc(s_nt, 1)

            def assign_slots(b):
                dve.wait_ge(p_start, b + 1)
                v.tensor_copy(tile_end[:, :], HT[0:E, H_END:H_END + 1])
                then(v.tensor_scalar(start[:, :], HT[:, H_START:H_START + E], float(P), -FAR, ALU.mult, ALU.add))
                lo, hi = FIRST[b] * CT, FIRST[b + 1] * CT
                then(v.tensor_tensor(key[:, lo:hi, :], key[:, lo:hi, :], bc(start[:, :].unsqueeze(1), P, hi - lo, E),
                                     ALU.add))
                for t in range(lo, hi):
                    ins = v.max(keys[:, t, :], key[:, t, :])
                then(ins)
                v.tensor_scalar(slots[:, lo * K:hi * K], flat(keys[:, lo:hi, :]), -1.0, None,
                                ALU.add).then_inc(s_slot, 1)
                v.tensor_scalar(ended[:, 0:ET[b]], iota_f[:, 0:ET[b]], tile_end[:, 0:1], None,
                                ALU.is_ge).then_inc(s_ended, 1)

            def weight_columns(b):
                dve.wait_ge(p_erow, b + 1)
                row = HT[0:1, 0:ET[b]]
                v.tensor_scalar(woff[0:1, 0, ET0[b]:ET0[b + 1]], row, float(E - 1), float(2 * I), ALU.min, ALU.mult)
                v.tensor_scalar(woff[0:1, 1, ET0[b]:ET0[b + 1]], row, float(E - 1), float(P), ALU.min,
                                ALU.mult).then_inc(s_woff, 1)

            dve.wait_ge(s_cact, 1)
            inverse_x(0)
            inverse_x(1)
            for k in range(NC + 3):
                front, mlp, route = k < NC, 1 <= k <= NC, 2 <= k < NC + 2
                c = k - 2
                if route:
                    inverse_v(c)
                if c >= 1 and c - 1 != EARLY:
                    mask_groups()
                if front:
                    ssm(k)
                if c >= 1 and c - 1 != EARLY:
                    choose(c - 1)
                if c == EARLY:
                    group_sums(c)
                if mlp:
                    hidden(k - 1, 0)
                    hidden(k - 1, 1)
                if c == EARLY:
                    group_seconds()
                    take_ranks(c - 1)
                    compare_groups()
                    mask_groups()
                    choose(c)
                    hidden(k - 1, 2)
                    hidden(k - 1, 3)
                    take_ranks(c)
                    count_tiles(0)
                    assign_slots(0)
                if front:
                    conv(k)
                if c >= 1 and c - 1 != EARLY and c != EARLY:
                    take_ranks(c - 1)
                    if c - 1 in LAST:
                        count_tiles(batch_of(c - 1))
                if mlp and c != EARLY:
                    hidden(k - 1, 2)
                if c - 1 in LAST[1:]:
                    assign_slots(batch_of(c - 1))
                if mlp and c != EARLY:
                    hidden(k - 1, 3)
                if route and c != EARLY:
                    group_sums(c)
                if front:
                    diagonal(k)
                if route and c != EARLY:
                    group_seconds()
                if k in (0, 2):
                    inverse_x(2 + k // 2)
                if mlp:
                    mlp_out(k - 1)
                if front:
                    norm2(k)
                if route and c != EARLY:
                    compare_groups()
                if c - 1 in LAST:
                    weight_columns(batch_of(c - 1))

            def is_at_least(q, n):
                return not isinstance(q, int) or q >= n

            def mul_h(q, u):
                r = u % 2
                dve.wait_ge(s_eg, q + 1)
                if is_at_least(q, 2):
                    dve.wait_ge(p_th, q - 1)
                v.tensor_tensor(
                    eh[:, r, :].rearrange("p (a t c) -> p a t c", a=2, t=2),
                    GU[:, 2 * r:2 * r + 2, 0:4 * I].rearrange("p a (t c) -> p a t c", c=2 * I)[:, :, :, I:2 * I],
                    eg[:, r, :].rearrange("p (a t c) -> p a t c", a=2, t=2), ALU.mult).then_inc(s_eh, 1)

            def take_h(q, u):
                dve.wait_ge(p_th, q + 1)
                if is_at_least(q, 2):
                    dve.wait_ge(p_eo, q - 1)
                v.tensor_copy(hT[0:I, u % 2, :], HT[0:I, :]).then_inc(s_ht, 1)

            def quad(q, u):
                if not (isinstance(q, int) and q + 1 >= NQ):
                    mul_h(q + 1, u + 1)
                take_h(q, u)

            wt3 = wtab[:, :].rearrange("p (k e) -> p k e", e=E)

            def slot_weights(t, n):
                one = bass.ds(t, 1)
                v.tensor_tensor(wt3, bc(key[:, one, :], P, K, E),
                                bc(keys[:, one, :].rearrange("p a k -> p k a"), P, K, E),
                                ALU.is_equal).then_inc(s_wk, 1)
                dve.wait_ge(s_wk, n + 1)
                v.tensor_tensor(wt3, wt3, bc(rw[:, one, :], P, K, E), ALU.mult).then_inc(s_wk, 1)
                dve.wait_ge(s_wk, n + 2)
                v.tensor_reduce(wk[:, bass.ds(t * K, K)], wt3, AX_X, ALU.add).then_inc(s_wk, 1)
                dve.wait_ge(s_wk, n + 3)

            def normalize_weights():
                w = wk[:, :].rearrange("p (t k) -> p t k", k=K)
                then(v.tensor_reduce(wsum[:, 0, :], w, AX_X, ALU.add))
                then(v.tensor_scalar(wsum[:, 0, :], wsum[:, 0, :], 1e-20, None, ALU.add))
                then(v.reciprocal(wsum[:, 1, :], wsum[:, 0, :]))
                then(v.tensor_scalar(wsum[:, 1, :], wsum[:, 1, :], ROUTED_SCALE, None, ALU.mult))
                then(v.tensor_tensor(w, w, bc(wsum[:, 1, :].unsqueeze(2), P, NT, K), ALU.mult))

            def add_row(t, k):
                c, i = t // CT, t % CT
                v.scalar_tensor_tensor(
                    out=x_all[:, t, :], in0=gbuf[:, c % 2, i, k, :], scalar=wk[:, t * K + k:t * K + k + 1],
                    in1=x1r[:, t, :] if k == 0 else x_all[:, t, :], op0=ALU.mult, op1=ALU.add).then_inc(s_acc, 1)

            def add_round(c, k):
                if k == 0:
                    dve.wait_ge(d_gat[c], 16 * CT * K)
                else:
                    dve.wait_ge(s_acc, CT * K * c + CT * k)
                for t in tiles(c):
                    add_row(t, k)

            taken = [0]

            def mean_variance(which):
                if taken[0]:
                    dve.wait_ge(s_cmv, taken[0])
                taken[0] += 1
                for i, t in enumerate(which):
                    ins = v.bn_stats(cst[:, i, :], x_all[:, t, :])
                then(ins)
                for i, t in enumerate(which):
                    ins = v.bn_aggr(cmv[:, t, :], cst[:, i, :])
                ins.then_inc(s_cmv, 1)

            def inverse_deviation(r):
                lo, hi = ROOTS[r]
                dve.wait_ge(s_csd, r + 1)
                then(v.reciprocal(csd[:, 1, lo:hi], csd[:, 0, lo:hi]))

            def normalize(which):
                for t in which:
                    ins = v.tensor_scalar(x_all[:, t, :], x_all[:, t, :], cmv[:, t, 0:1], csd[:, 1, t:t + 1],
                                          ALU.subtract, ALU.mult)
                ins.then_inc(s_out, 1)

            mul_h(0, 0)
            for q in range(UN):
                quad(q, q)
                if q % 2:
                    slot_weights(q // 2, 3 * (q // 2))
            with dve.Fori(1, NT // WT) as i:
                for u in range(UN):
                    quad(i * UN + u, u)
                    if u % 2:
                        slot_weights(i * WT + u // 2, i * (3 * WT) + 3 * (u // 2))
            normalize_weights()
            if SUM_AT[0] > NT // WT:
                with dve.Fori(NT // WT, SUM_AT[0]) as i:
                    for u in range(UN):
                        quad(i * UN + u, u)
            for c, turn in enumerate(SUM_AT):
                for k in range(K):
                    quad(turn * UN + k, turn * UN + k)
                    add_round(c, k)
                nxt = (SUM_AT + (NQ // UN - 1,))[c + 1]
                if turn + K // UN < nxt:
                    with dve.Fori(turn + K // UN, nxt) as i:
                        for u in range(UN):
                            quad(i * UN + u, u)
            for q in range(max(NQ - UN, (SUM_AT[-1] + K // UN) * UN), NQ):
                quad(q, q)
            def shared_hidden(c, j):
                dve.wait_ge(s_ssil, SJ * c + j + 1)
                if c:
                    dve.wait_ge(p_sd, c)
                v.tensor_tensor(hs[0:I, j, :], GU[0:I, 2 * j + 1, :], ssil[0:I, j, :], ALU.mult).then_inc(s_sh, 1)

            def add_shared(c):
                acc = x_all if c < SUMMED else x1r
                dve.wait_ge(p_sd, c + 1)
                if c < SUMMED:
                    dve.wait_ge(s_acc, CT * K * (c + 1))
                v.tensor_tensor(flat(acc[:, span(c), :]), (HT if c % 2 else OT)[:, :], flat(acc[:, span(c), :]),
                                ALU.add).then_inc(s_res, 1)

            for c in range(NC):
                shared_hidden(c, 0)
                shared_hidden(c, 1)
                if c in ROUNDS:
                    summed, first = ROUNDS[c]
                    for k in range(first, first + HALF):
                        add_round(summed, k)
                for n in STATS.get(c, ()):
                    dve.wait_ge(s_res, n + 1)
                    mean_variance(tiles(n))
                if c == NC - 1:
                    inverse_deviation(0)
                    v.scalar_tensor_tensor(out=csd[:, 2, 0:SUMMED * CT], in0=cmv[:, 0:SUMMED * CT, 0], scalar=-1.0,
                                           in1=csd[:, 1, 0:SUMMED * CT], op0=ALU.mult,
                                           op1=ALU.mult).then_inc(s_ncmean, 1)
                    dve.wait_ge(s_res, SUMMED + 1)
                    for k in range(K):
                        add_round(SUMMED, k)
                add_shared(c)
            dve.wait_ge(s_acc, CT * K * (SUMMED + 1))
            mean_variance(tiles(SUMMED))
            dve.wait_ge(s_res, NC)
            for i, t in enumerate(tiles(NC - 1)):
                for k in range(K):
                    if k % HALF == 0:
                        dve.wait_ge(d_gat_half[2 * i + k // HALF], 16 * HALF)
                    add_row(t, k)
                    dve.wait_ge(s_acc, (t * K) + k + 1)
                mean_variance([t])
                inverse_deviation(i + 1)
                normalize([t - 1] if i else tiles(SUMMED))
            inverse_deviation(CT + 1)
            normalize([NT - 1])


def kernel(**inputs):
    import numpy as np
    import concourse.bacc as bacc
    from concourse.bass_utils import run_bass_kernel_spmd as run

    g = {k[3:]: np.asarray(a) for k, a in inputs.items()}
    a = lambda n: g["attn_" + n]
    f = lambda n: g["ffn_" + n]
    cols = [a("norm_w"), *a("conv_w")[:, 0, :].T, a("conv_b"), a("a"), a("b"), a("mlp_norm_w"),
            *a("b_gate").reshape(NM, P), *a("b_up").reshape(NM, P)]
    ins = {
        "x": a("x"),
        "vecs": np.stack(cols, axis=1),
        "w_gate": a("w_gate"),
        "w_up": a("w_up"),
        "w_down": a("w_down"),
        "b_down": a("b_down"),
        "gate_wT": f("gate_w").T,
        "gate_bias": f("gate_bias"),
        "wgu": np.concatenate([f("Wg"), f("Wu")], axis=1).transpose(2, 0, 1).reshape(P, E * 2 * I),
        "wd": f("Wd").transpose(2, 0, 1).reshape(I, E * P),
        "sgu": np.stack([f("Sg"), f("Su")]).reshape(2, SJ, I, P).transpose(3, 0, 1, 2),
        "sd": f("Sd").T.reshape(SJ, I, P).transpose(1, 0, 2),
    }
    ins = {n: np.ascontiguousarray(v) for n, v in ins.items()}
    nc = bacc.Bacc("TRN2", target_bir_lowering=False, num_devices=1)
    aps = {n: nc.dram_tensor(n + "_dram", v.shape, mybir.dt.from_np(v.dtype), kind="ExternalInput").ap()
           for n, v in ins.items()}
    out = nc.dram_tensor("out_dram", (NB, T, P), F32, kind="ExternalOutput").ap()
    xs = [nc.dram_tensor(f"xs{b}_dram", (ET[b] * P, P), F32, kind="Internal").ap() for b in range(NBAT)]
    os = [nc.dram_tensor(f"os{b}_dram", (ET[b] * P, P), F32, kind="Internal").ap() for b in range(NBAT)]
    build(nc, out=out, xs=xs, os=os, **aps)
    r = run(nc, [{n + "_dram": v for n, v in ins.items()}], core_ids=[0])
    return r.results[0]["out_dram"]
```
